# Optimizing a Trainium2 kernel written in Bass

```python
import numpy as np
import jax
import jax.numpy as jnp

def _softmax(x, axis=-1):
    return jax.nn.softmax(x, axis=axis)

def _gelu(x):
    return jax.nn.gelu(x, approximate=True)

def _silu(x):
    return jax.nn.silu(x)

def _sigmoid(x):
    return jax.nn.sigmoid(x)

def _layernorm(x, axis=-1, eps=1e-05):
    m = jnp.mean(x, axis=axis, keepdims=True)
    v = jnp.var(x, axis=axis, keepdims=True)
    return (x - m) / jnp.sqrt(v + eps)

def _scatter_add(tgt, idx, src, axis=0):
    return tgt.at[idx].add(src)

def _segment_sum(src, seg, n):
    return jax.ops.segment_sum(src, seg, n)
kernel_name = 'mk_adaln_ffn_d1_seqx_r4_41576d'

def setup_inputs(seed: int=0):
    np.random.seed(seed)
    _w = jnp.asarray

    def _rec_inputs():
        import jax
        import jax.numpy as jnp
        _rk = jax.random.key(seed)
        x = -7.109e-05 + 0.9999 * jax.random.normal(jax.random.fold_in(_rk, 1), (2, 1024, 256), jnp.float32)
        _lenS = 1024 - jax.random.randint(jax.random.fold_in(_rk, 7), (2,), 0, max(1, 1024 // 4) + 1, jnp.int32)
        _lenS2 = 1024 - jax.random.randint(jax.random.fold_in(_rk, 8), (2,), 0, max(1, 1024 // 4) + 1, jnp.int32)
        cond_1024 = -0.00356592 + 0.997978 * jax.random.normal(jax.random.fold_in(_rk, 11), (2, 256), jnp.float32)
        return (x, cond_1024)
    x, cond_1024 = _rec_inputs()

    def _L0_cond_setup():
        import jax, jax.numpy as jnp
        import numpy as np
        N, T, D, H = (128, 128, 256, 256)
        key = jax.random.key(seed)
        k1, k2, k3, k4 = jax.random.split(key, 4)
        x = jax.random.normal(k1, (N, T, D), dtype=jnp.float32)
        h0 = jax.random.normal(k2, (N, H), dtype=jnp.float32)
        Wx = jax.random.normal(k3, (D, H), dtype=jnp.float32) / np.sqrt(D)
        Wh = jax.random.normal(k4, (H, H), dtype=jnp.float32) / np.sqrt(H)
        b = jnp.zeros((H,), dtype=jnp.float32)
        return {'x': x, 'h0': h0, 'Wx': Wx, 'Wh': Wh, 'b': b}
    _L0_cond_all = _L0_cond_setup()
    _L0_cond_in = {k: v for k, v in _L0_cond_all.items() if k in ('Wx', 'Wh', 'b')}
    del _L0_cond_all

    def _L0_ffn_setup():
        import jax, jax.numpy as jnp
        import numpy as np
        D_MODEL = 256
        N_EXPERTS = 8
        TOP_K = 2
        HIDDEN = 4 * D_MODEL
        key = jax.random.key(seed)
        ks = jax.random.split(key, 6)
        B, S = (2, 512)
        x = jax.random.normal(ks[0], (B, S, D_MODEL), dtype=jnp.float32)
        shared_w1 = jax.random.normal(ks[1], (HIDDEN, D_MODEL), dtype=jnp.float32) * 0.02
        shared_w2 = jax.random.normal(ks[2], (D_MODEL, HIDDEN), dtype=jnp.float32) * 0.02
        experts_w1 = jax.random.normal(ks[3], (N_EXPERTS, HIDDEN, D_MODEL), dtype=jnp.float32) * 0.02
        experts_w2 = jax.random.normal(ks[4], (N_EXPERTS, D_MODEL, HIDDEN), dtype=jnp.float32) * 0.02
        gate_w = jax.random.normal(ks[5], (N_EXPERTS, D_MODEL), dtype=jnp.float32) * 0.02
        return {'x': x, 'shared_w1': shared_w1, 'shared_w2': shared_w2, 'experts_w1': experts_w1, 'experts_w2': experts_w2, 'gate_w': gate_w}
    _L0_ffn_all = _L0_ffn_setup()
    _L0_ffn_in = {k: v for k, v in _L0_ffn_all.items() if k in ('shared_w1', 'shared_w2', 'experts_w1', 'experts_w2', 'gate_w')}
    del _L0_ffn_all
    return {'x': x, 'cond_1024': cond_1024, 'L0_cond_Wx': _L0_cond_in['Wx'], 'L0_cond_Wh': _L0_cond_in['Wh'], 'L0_cond_b': _L0_cond_in['b'], 'L0_ffn_shared_w1': _L0_ffn_in['shared_w1'], 'L0_ffn_shared_w2': _L0_ffn_in['shared_w2'], 'L0_ffn_experts_w1': _L0_ffn_in['experts_w1'], 'L0_ffn_experts_w2': _L0_ffn_in['experts_w2'], 'L0_ffn_gate_w': _L0_ffn_in['gate_w']}

def reference(x, cond_1024, L0_cond_Wx, L0_cond_Wh, L0_cond_b, L0_ffn_shared_w1, L0_ffn_shared_w2, L0_ffn_experts_w1, L0_ffn_experts_w2, L0_ffn_gate_w):
    import jax
    import jax.numpy as jnp

    def _L0_cond_ref(x, h0, Wx, Wh, b):
        import jax, jax.numpy as jnp
        import numpy as np
        N, T, D, H = (128, 128, 256, 256)
        xp = jnp.einsum('ntd,dh->nth', x, Wx) + b

        def step(prev_h, xp_t):
            next_h = jnp.tanh(xp_t + prev_h @ Wh)
            return (next_h, next_h)
        _, h = jax.lax.scan(step, h0, jnp.swapaxes(xp, 0, 1))
        return jnp.swapaxes(h, 0, 1)

    def _L0_ffn_ref(x, shared_w1, shared_w2, experts_w1, experts_w2, gate_w):
        import jax, jax.numpy as jnp
        import numpy as np
        D_MODEL = 256
        N_EXPERTS = 8
        TOP_K = 2
        HIDDEN = 4 * D_MODEL
        B, S, D = x.shape
        T = B * S
        x_flat = x.reshape(T, D)
        shared = jnp.einsum('td,dh->th', x_flat, shared_w1.T)
        shared = jnp.einsum('th,hd->td', jax.nn.silu(shared), shared_w2.T)
        gate_logits = x_flat @ gate_w.T
        top_k_gates, top_k_idx = jax.lax.top_k(gate_logits, TOP_K)
        top_k_gates = jax.nn.softmax(top_k_gates, axis=1)
        gates = jnp.zeros((T, N_EXPERTS), dtype=x.dtype)
        gates = gates.at[jnp.arange(T)[:, None], top_k_idx].set(top_k_gates)
        h = jnp.einsum('td,ehd->teh', x_flat, experts_w1)
        expert_out = jnp.einsum('teh,edh->ted', jax.nn.silu(h), experts_w2)
        selected = jnp.einsum('ted,te->td', expert_out, gates)
        return (shared + selected).reshape(B, S, D)
    x = x + _L0_ffn_ref(_L0_cond_ref(x, cond_1024, L0_cond_Wx, L0_cond_Wh, L0_cond_b), L0_ffn_shared_w1, L0_ffn_shared_w2, L0_ffn_experts_w1, L0_ffn_experts_w2, L0_ffn_gate_w)
    return x

_drawn_inputs = setup_inputs


def setup_inputs(seed=0):
    import zlib

    import numpy as np

    out = dict(_drawn_inputs(seed))
    spreads = {'L0_cond_b': (0.0, 0.395)}
    factors = {'cond_1024': 8.0}
    for name, (base, spread) in spreads.items():
        noise = np.random.default_rng([zlib.crc32(name.encode()), seed]).standard_normal(out[name].shape)
        drawn = base * np.exp(spread * noise) if base else spread * noise
        out[name] = jnp.asarray(drawn.astype(out[name].dtype))
    for name, factor in factors.items():
        out[name] = (out[name] * factor).astype(out[name].dtype)
    return out
```

```python
from contextlib import ExitStack

import numpy as np

import concourse.bass as bass
from concourse import mybir

F32 = mybir.dt.float32
U32 = mybir.dt.uint32
ALU = mybir.AluOpType
ACT = mybir.ActivationFunctionType
AX = mybir.AxisListType

P = 128
B, T, D = 2, 1024, 256
HID = 1024
E = 8
TOP = 2
K = D // P
Q = HID // P
NTOK = B * T

C = P // B
L = T // C
COLS = C * B
SPECULATIVE_ROUNDS = 3
TOLERANCE = 2.0 ** -18
EXPECTED_SAME = P * K * (COLS - B)

TILES = NTOK // P
SLOT_TILES = (TOP * NTOK + E * (P - 1)) // P
ALL_TILES = TILES + SLOT_TILES
ROW = D + 2
BANK = 512
HALVES = HID // BANK
TPB = BANK // P
WCOLS = K * HID + Q * D
RING = 4
SORT_FROM = RING
SORT_TILES = TILES // 2


def build(nc, x_cols, x_rows, h0_cols, wx, wh, bias, weights, gate_cols, out):
    ctx = ExitStack()
    with ctx:
        def sb(name, shape, dt=F32):
            return ctx.enter_context(nc.sbuf_tensor(name, shape, dt))

        def sem(name):
            return ctx.enter_context(nc.semaphore(name))

        sorted_rows = nc.dram_tensor("sorted_rows", [SLOT_TILES * P, ROW], F32).ap()

        w_all = sb("w_all", [P, E + 1, WCOLS])
        states = sb("states", [P, K, L + 1, COLS])
        space = sb("space", [P, 2 * K * NTOK])
        xT = space[:, 0:K * NTOK].rearrange("p (k n) -> p k n", k=K)
        xproj = space[:, K * NTOK:2 * K * NTOK].rearrange("p (k n) -> p k n", k=K)
        wx_sb = sb("wx_sb", [P, K, D])
        wh_sb = sb("wh_sb", [P, K, D])
        bias_sb = sb("bias_sb", [P, K])
        gate_sb = sb("gate_sb", [P, K, E])
        identity = sb("identity", [P, P])
        before = sb("before", [P, P])
        ones = sb("ones", [P, P])
        pad_row = sb("pad_row", [P, ROW])
        iota_e = sb("iota_e", [P, E])
        iota_full = sb("iota_full", [P, TILES])
        iota_tile = sb("iota_tile", [P, SLOT_TILES])
        token_no = sb("token_no", [P, TILES])
        same_count = sb("same_count", [P, 1])
        same_count_u = sb("same_count_u", [P, 1], U32)
        xin = sb("xin", [P, 2, K, P])

        at = [0]

        def carve(*shape):
            n = int(np.prod(shape))
            v = space[:, at[0]:at[0] + n]
            at[0] += n
            assert at[0] <= 2 * K * NTOK
            if len(shape) == 1:
                return v
            if len(shape) == 2:
                return v.rearrange("p (a b) -> p a b", a=shape[0])
            return v.rearrange("p (a b c) -> p a b c", a=shape[0], b=shape[1])

        hr = carve(RING, TOP, ROW)
        hidden = carve(HID)
        hiddenT = carve(Q, P)
        ys = carve(RING, D)
        x_res = carve(2, D)
        slots_u = carve(TILES, TOP).bitcast(U32)
        meta = carve(TILES, TOP, 2)
        expert_u = carve(SLOT_TILES).bitcast(U32)
        slot_idx = carve(RING, TOP).bitcast(U32)
        token_idx = carve(RING).bitcast(U32)
        n_drift = K * (COLS - B)
        drift = hidden[:, 0:n_drift].rearrange("p (k n) -> p k n", k=K)
        drift_ok = hidden[:, n_drift:2 * n_drift].rearrange("p (k n) -> p k n", k=K)
        routing_at = at[0]
        xs = carve(RING, ROW)
        at[0] = routing_at
        logits = carve(TILES, E)
        best = carve(TILES, E)
        best_at = carve(TILES, E).bitcast(U32)
        chosen = carve(TOP, TILES)
        gap = carve(TILES)
        exp_gap = carve(TILES)
        denom = carve(TILES)
        onehot = carve(TOP, TILES, E)
        picked = carve(TILES, E)
        earlier = carve(E, TILES)
        per_tile = carve(E, TILES)
        running = carve(E, TILES)
        restart = carve(E, TILES)
        slot_of = carve(E, TILES)
        masked = carve(TOP * TILES, E)
        filled = carve(E, TILES)
        tiles_of = carve(E)
        tiles_upto = carve(E)
        base = carve(E)
        slots = carve(TOP, TILES)
        ended = carve(SLOT_TILES, E)
        expert_of = carve(SLOT_TILES)

        Z = [[ctx.enter_context(nc.psum_tensor(f"z{p}{m}", [P, BANK], F32)) for m in range(K)] for p in range(2)]
        TR = [ctx.enter_context(nc.psum_tensor(f"tr{h}", [P, BANK], F32)) for h in range(HALVES)]
        PY = ctx.enter_context(nc.psum_tensor("py", [P, BANK], F32))
        PX = ctx.enter_context(nc.psum_tensor("px", [P, BANK], F32))

        wx_in, wh_in, x_in = sem("wx_in"), sem("wh_in"), [sem(f"x_in{k}") for k in range(K)]
        bias_in, h0_in, gate_in = sem("bias_in"), sem("h0_in"), sem("gate_in")
        w_in = [sem(f"w_in{e}") for e in range(E + 1)]
        x_res_in = [sem(f"x_res_in{u}") for u in range(2)]
        xs_in = [sem(f"xs_in{u}") for u in range(RING)]
        consts = sem("consts")
        identity_ok, pad_ok = sem("identity_ok"), sem("pad_ok")
        xproj_mm, xproj_ok = sem("xproj_mm"), sem("xproj_ok")
        start_ok = sem("start_ok")
        z_mm = [sem(f"z_mm{m}") for m in range(K)]
        h_ok = [sem(f"h_ok{k}") for k in range(K)]
        start_ok_general = sem("start_ok_general")
        z_mm_general = [sem(f"z_mm_general{m}") for m in range(K)]
        h_ok_general = [sem(f"h_ok_general{k}") for k in range(K)]
        check_chain, drift_counted, drift_summed, drift_known = sem("check_chain"), sem("drift_counted"), sem("drift_summed"), sem("drift_known")
        recurrence_over = sem("recurrence_over")
        logits_mm, gap_ok, exp_ok, picked_ok, prefix_mm, prefix_read, routed = (
            sem(n) for n in "logits_mm gap_ok exp_ok picked_ok prefix_mm prefix_read routed".split())
        chain = sem("chain")
        xin_ok, up_mm, hidden_ok, tr_mm, hiddenT_ok, down_mm, y_ok = (
            sem(n) for n in "xin_ok up_mm hidden_ok tr_mm hiddenT_ok down_mm y_ok".split())
        row_mm, row_ok, row_copied = sem("row_mm"), sem("row_ok"), sem("row_copied")
        sorted_ok = [sem(f"sorted_ok{u}") for u in range(RING)]
        xs_mm, idx_ok = sem("xs_mm"), sem("idx_ok")
        summed, stored = sem("summed"), [sem(f"stored{u}") for u in range(RING)]
        added = sem("added")
        padded, padded_out = sem("padded"), sem("padded_out")
        pool_waited, sp_waited = sem("pool_waited"), sem("sp_waited")
        block = ctx.enter_context(nc.Block())

        GENERAL_ROUNDS = C - SPECULATIVE_ROUNDS

        def column(k, j):
            return states[:, k, bass.ds(j, 1), :].rearrange("p a n -> p (a n)")

        def weight(e, at, n):
            return w_all[:, bass.ds(e, 1), at:at + n].rearrange("p a n -> p (a n)")

        @block.sync
        def _(sp):
            sp.dma_start(wx_sb[:], wx).then_inc(wx_in, 16)
            for k in range(K):
                sp.dma_start(xT[:, k], x_cols[k]).then_inc(x_in[k], 16)
            sp.dma_start(bias_sb[:], bias).then_inc(bias_in, 16)
            sp.dma_start(wh_sb[:], wh).then_inc(wh_in, 16)
            sp.dma_start(states[:, :, 0, 0:B], h0_cols).then_inc(h0_in, 16)
            sp.dma_start(gate_sb[:], gate_cols).then_inc(gate_in, 16)
            for e in (E, *range(E)):
                sp.dma_start(w_all[:, e], weights[e]).then_inc(w_in[e], 16)
            sp.wait_ge(pad_ok, 3)
            sp.dma_start(sorted_rows.rearrange("(t p) r -> p t r", p=P),
                         pad_row[:].unsqueeze(1).broadcast_to([P, SLOT_TILES, ROW])).then_inc(padded, 16)
            sp.dma_start(out[NTOK:NTOK + P, :], pad_row[:, 0:D]).then_inc(padded_out, 16)
            sp.wait_ge(recurrence_over, 1)
            x_tiles = x_rows.rearrange("(t p) d -> t p d", p=P)
            out_tiles = out.rearrange("(t p) d -> t p d", p=P)

            def tile_of(dram, t):
                return dram[bass.ds(t, 1), :, :].rearrange("a p d -> (a p) d")

            for g in range(2):
                sp.dma_start(x_res[:, g], x_tiles[g]).then_inc(x_res_in[g], 16)

            def store(g, u, more):
                sp.wait_ge(summed, g + 1)
                sp.dma_start(tile_of(out_tiles, g), ys[:, u]).then_inc(stored[u], 16)
                if more:
                    sp.dma_start(x_res[:, u % 2], tile_of(x_tiles, g + 2)).then_inc(x_res_in[u % 2], 16)

            with sp.Fori(0, TILES // RING - 1) as i:
                for u in range(RING):
                    store(i * RING + u, u, True)
            sorted_tiles = sorted_rows.rearrange("(t p) r -> t p r", p=P)

            def load(t, u, refill):
                if refill:
                    sp.wait_ge(y_ok, t + (TILES - RING + 1))
                    sp.sem_inc(sp_waited, 1)
                    sp.wait_ge(idx_ok, t - RING + 1)
                sp.dma_start(xs[:, u], tile_of(sorted_tiles, t)).then_inc(xs_in[u], 16)

            for u in range(RING):
                sp.wait_ge(sorted_ok[u], 16 * TOP * TILES // RING)
            for t in range(RING):
                load(t, t, False)
            for u in range(RING):
                store(TILES - RING + u, u, u < RING - 2)
            with sp.Fori(1, SLOT_TILES // RING) as i:
                for u in range(RING):
                    load(i * RING + u, u, True)
            for t in range(SLOT_TILES // RING * RING, SLOT_TILES):
                load(t, t % RING, True)
            sp.wait_ge(added, 16 * SLOT_TILES)

        @block.gpsimd
        def _(pool):
            nc.gpsimd.memset(identity[:], 0.0).then_inc(identity_ok, 1)
            nc.gpsimd.memset(before[:], 1.0).then_inc(identity_ok, 1)
            nc.gpsimd.memset(pad_row[:], 0.0).then_inc(pad_ok, 1)
            nc.gpsimd.memset(ones[:], 1.0).then_inc(consts, 1)
            pool.wait_ge(identity_ok, 2)
            nc.gpsimd.affine_select(out=identity[:], in_=identity[:], compare_op=ALU.not_equal, fill=1.0,
                                    base=0, pattern=[[-1, P]], channel_multiplier=1).then_inc(identity_ok, 1)
            nc.gpsimd.affine_select(out=before[:], in_=before[:], compare_op=ALU.is_gt, fill=0.0,
                                    base=0, pattern=[[1, P]], channel_multiplier=-1).then_inc(consts, 1)
            for to, pattern, start, per_partition in (
                    (iota_e[:], [[1, E]], 0, 0), (iota_full[:], [[P, TILES]], 0, 0),
                    (iota_tile[:], [[1, SLOT_TILES]], 0, 0), (token_no[:], [[P, TILES]], 0, 1)):
                nc.gpsimd.iota(to, pattern=pattern, base=start, channel_multiplier=per_partition,
                               allow_small_or_imprecise_dtypes=True).then_inc(consts, 1)
            pool.wait_ge(pad_ok, 1)
            nc.gpsimd.iota(pad_row[:, D:D + 1], pattern=[[1, 1]], base=NTOK, channel_multiplier=1,
                           allow_small_or_imprecise_dtypes=True).then_inc(pad_ok, 2)

            def waited(semaphore, value):
                pool.wait_ge(semaphore, value)
                pool.sem_inc(pool_waited, 1)

            pool.wait_ge(routed, 1)

            def sort(t, u):
                waited(row_ok, t + 1)
                nc.gpsimd.tensor_copy(hr[:, u, 1, 0:D], hr[:, u, 0, 0:D]).then_inc(row_copied, 1)
                nc.gpsimd.tensor_copy(hr[:, u, :, D:ROW], meta[:, bass.ds(t, 1)].rearrange("p a k c -> p (a k) c")).then_inc(row_copied, 1)
                nc.gpsimd.tensor_copy(slot_idx[:, u], slots_u[:, bass.ds(t, 1)].rearrange("p a k -> p (a k)")).then_inc(row_copied, 1)
                waited(row_copied, t * 3 + 3)
                for k in range(TOP):
                    nc.gpsimd.indirect_dma_start(
                        out=sorted_rows, out_offset=bass.IndirectOffsetOnAxis(slot_idx[:, u, k:k + 1], 0),
                        in_=hr[:, u, k], in_offset=None).then_inc(sorted_ok[u], 16)

            pool.wait_ge(padded, 16)
            for t in range(RING):
                sort(t, t)
            with pool.Fori(1, TILES // RING) as i:
                for u in range(RING):
                    waited(sorted_ok[u], i * (16 * TOP))
                    sort(i * RING + u, u)

            def add(t, u):
                waited(idx_ok, t + 1)
                waited(y_ok, t + (TILES + 1))
                nc.gpsimd.indirect_dma_start(
                    out=out, out_offset=bass.IndirectOffsetOnAxis(token_idx[:, u:u + 1], 0),
                    in_=ys[:, u], in_offset=None, compute_op=ALU.add).then_inc(added, 16)
                waited(added, t * 16 + 16)

            pool.wait_ge(padded_out, 16)
            for u in range(RING):
                pool.wait_ge(stored[u], 16 * TILES // RING)
            with pool.Fori(0, SLOT_TILES // RING) as i:
                for u in range(RING):
                    add(i * RING + u, u)
            for t in range(SLOT_TILES // RING * RING, SLOT_TILES):
                add(t, t % RING)

        @block.vector
        def _(dve):
            links = [0]

            def link(instruction):
                links[0] += 1
                instruction.then_inc(chain, 1)
                dve.wait_ge(chain, links[0])

            nc.vector.memset(states[:, :, 0, B:COLS], 0.0).then_inc(start_ok, 1)

            def next_start(h, count, started):
                for k in range(K):
                    dve.wait_ge(h[k], count)
                nc.vector.tensor_copy(states[:, :, 0, B:COLS], states[:, :, L, 0:COLS - B]).then_inc(started, 1)

            for r in range(1, SPECULATIVE_ROUNDS):
                next_start(h_ok, r * L, start_ok)

            for k in range(K):
                dve.wait_ge(h_ok[k], SPECULATIVE_ROUNDS * L)
            link(nc.vector.tensor_sub(drift, states[:, :, L, 0:COLS - B], states[:, :, 0, B:COLS]))
            link(nc.vector.tensor_mul(drift_ok, drift, drift))
            link(nc.vector.tensor_scalar(drift, drift_ok, TOLERANCE ** 2, None, ALU.is_le))
            nc.vector.tensor_reduce(same_count[:], drift, AX.XY, ALU.add).then_inc(drift_counted, 1)
            dve.wait_ge(drift_summed, 1)
            nc.vector.tensor_copy(same_count_u[:], PY[:, 0:1]).then_inc(drift_known, 1)
            dve.wait_ge(drift_known, 1)
            same = dve.value_load(same_count_u[0:1, 0:1], min_val=0, max_val=EXPECTED_SAME)
            with dve.If(same != EXPECTED_SAME):
                next_start(h_ok, SPECULATIVE_ROUNDS * L, start_ok_general)
                with dve.Fori(1, GENERAL_ROUNDS) as r:
                    next_start(h_ok_general, r * L, start_ok_general)
            dve.engine_nop()

            dve.wait_ge(logits_mm, 1)
            link(nc.vector.tensor_copy(logits, PX[:, 0:TILES * E].rearrange("p (t e) -> p t e", e=E)))
            for t in range(TILES):
                last = nc.vector.max(best[:, t], logits[:, t])
            link(last)
            nc.vector.tensor_sub(gap, best[:, :, 1], best[:, :, 0]).then_inc(gap_ok, 1)
            for t in range(TILES):
                last = nc.vector.max_index(best_at[:, t], best[:, t], logits[:, t])
            link(last)
            for k in range(TOP):
                last = nc.vector.tensor_copy(chosen[:, k], best_at[:, :, k])
            link(last)
            dve.wait_ge(consts, 6)
            for k in range(TOP):
                last = nc.vector.tensor_tensor(
                    onehot[:, k], chosen[:, k].unsqueeze(2).broadcast_to([P, TILES, E]),
                    iota_e[:].unsqueeze(1).broadcast_to([P, TILES, E]), ALU.is_equal)
            link(last)
            nc.vector.tensor_add(picked, onehot[:, 0], onehot[:, 1]).then_inc(picked_ok, 1)
            link(nc.vector.memset(restart, 1.0))
            link(nc.vector.memset(restart[:, :, 0:1], 0.0))
            dve.wait_ge(exp_ok, 1)
            link(nc.vector.tensor_scalar_add(denom, exp_gap, 1.0))
            link(nc.vector.reciprocal(meta[:, :, 0, 1], denom))
            nc.vector.tensor_mul(meta[:, :, 1, 1], exp_gap, meta[:, :, 0, 1])
            for k in range(TOP):
                nc.vector.tensor_copy(meta[:, :, k, 0], token_no[:])
            dve.wait_ge(prefix_mm, 1)
            nc.vector.tensor_copy(earlier, PX[:, P:2 * P].rearrange("p (t e) -> p e t", e=E))
            prefix = nc.vector.tensor_copy(per_tile, PX[:, 2 * P:3 * P].rearrange("p (t e) -> p e t", e=E))
            prefix.then_inc(prefix_read, 1)
            dve.wait_ge(prefix_read, 1)
            flat = lambda v: v.rearrange("p e t -> p (e t)")
            link(nc.vector.tensor_tensor_scan(flat(running), flat(restart), flat(per_tile), 0.0, ALU.mult, ALU.add))
            link(nc.vector.tensor_tensor(filled, running[:, :, TILES - 1:TILES].broadcast_to([P, E, TILES]),
                                         iota_full[:].unsqueeze(1).broadcast_to([P, E, TILES]), ALU.is_gt))
            link(nc.vector.tensor_reduce(tiles_of, filled, AX.X, ALU.add))
            link(nc.vector.tensor_tensor_scan(tiles_upto, ones[:, 0:E], tiles_of, 0.0, ALU.mult, ALU.add))
            nc.vector.tensor_tensor(ended, tiles_upto.unsqueeze(1).broadcast_to([P, SLOT_TILES, E]),
                                    iota_tile[:].unsqueeze(2).broadcast_to([P, SLOT_TILES, E]), ALU.is_le)
            link(nc.vector.tensor_sub(base, tiles_upto, tiles_of))
            link(nc.vector.tensor_reduce(expert_of, ended, AX.X, ALU.add))
            nc.vector.tensor_scalar_min(expert_u, expert_of, float(E - 1))
            link(nc.vector.tensor_scalar_mul(tiles_upto, base, float(P)))
            link(nc.vector.tensor_sub(slot_of, running, per_tile))
            link(nc.vector.tensor_add(slot_of, slot_of, earlier))
            link(nc.vector.tensor_add(slot_of, slot_of, tiles_upto.unsqueeze(2).broadcast_to([P, E, TILES])))
            for k in range(TOP):
                last = nc.vector.tensor_mul(masked[:, k * TILES:(k + 1) * TILES], onehot[:, k], slot_of.rearrange("p e t -> p t e"))
            link(last)
            link(nc.vector.tensor_reduce(slots.rearrange("p k t -> p (k t)"), masked, AX.X, ALU.add))
            for k in range(TOP):
                last = nc.vector.tensor_copy(slots_u[:, :, k], slots[:, k])
            last.then_inc(routed, 1)

            def residual(g, u, n):
                dve.wait_ge(x_res_in[u % 2], n)
                dve.wait_ge(y_ok, g + 1)
                nc.vector.tensor_add(ys[:, u], ys[:, u], x_res[:, u % 2]).then_inc(summed, 1)

            with dve.Fori(0, TILES // RING) as i:
                for u in range(RING):
                    residual(i * RING + u, u, i * (16 * RING // 2) + 16 * (u // 2 + 1))

            def index(t, u, n, again):
                dve.wait_ge(xs_in[u], n)
                if again:
                    dve.wait_ge(added, (t - RING + 1) * 16)
                nc.vector.tensor_copy(token_idx[:, u:u + 1], xs[:, u, D:D + 1]).then_inc(idx_ok, 1)

            for t in range(RING):
                index(t, t, 16, False)
            with dve.Fori(1, SLOT_TILES // RING) as i:
                for u in range(RING):
                    index(i * RING + u, u, i * 16 + 16, True)
            for t in range(SLOT_TILES // RING * RING, SLOT_TILES):
                index(t, t % RING, 16 * (t // RING + 1), True)

        @block.scalar
        def _(act):
            act.wait_ge(bias_in, 16)
            for n in range(NTOK // BANK):
                for m in range(K):
                    act.wait_ge(xproj_mm, n * K + m + 1)
                    nc.scalar.activation(xproj[:, m, n * BANK:(n + 1) * BANK], Z[n % 2][m][:], ACT.Identity,
                                         bias=bias_sb[:, m:m + 1]).then_inc(xproj_ok, 1)

            def steps(z, h, r):
                with act.Fori(0, L // 2) as i:
                    for u in range(2):
                        for m in range(K):
                            act.wait_ge(z[m], i * 2 + (r * L + u + 1))
                            nc.scalar.activation(column(m, i * 2 + u + 1), Z[u][m][:, 0:COLS], ACT.Tanh).then_inc(h[m], 1)

            for r in range(SPECULATIVE_ROUNDS):
                steps(z_mm, h_ok, r)
            for k in range(K):
                act.wait_ge(h_ok[k], SPECULATIVE_ROUNDS * L)
            act.wait_ge(drift_known, 1)
            same = act.value_load(same_count_u[0:1, 0:1], min_val=0, max_val=EXPECTED_SAME)
            with act.If(same != EXPECTED_SAME):
                with act.Fori(0, GENERAL_ROUNDS) as r:
                    steps(z_mm_general, h_ok_general, r)
                for k in range(K):
                    act.wait_ge(h_ok_general[k], GENERAL_ROUNDS * L)

            def shared_rows(g, u):
                nc.scalar.copy(xin[:, u % 2], states[:, :, bass.ds(g + 1, 1), :].rearrange("p k a n -> p k (a n)")).then_inc(xin_ok, 1)

            for g in range(2):
                shared_rows(g, g)
            act.wait_ge(gap_ok, 1)
            nc.scalar.activation(exp_gap, gap, ACT.Exp).then_inc(exp_ok, 1)

            def silu(g, p):
                for h in range(HALVES):
                    act.wait_ge(up_mm, g * HALVES + (h + 1))
                    if h == 0 and not (isinstance(g, int) and g == 0):
                        act.wait_ge(tr_mm, g * HALVES)
                    nc.scalar.activation(hidden[:, h * BANK:(h + 1) * BANK], Z[p][h][:], ACT.Silu).then_inc(hidden_ok, 1)

            def transposed(g):
                for h in range(HALVES):
                    act.wait_ge(tr_mm, g * HALVES + (h + 1))
                    if h == 0 and not (isinstance(g, int) and g == 0):
                        act.wait_ge(down_mm, g)
                    nc.scalar.copy(hiddenT[:, h * TPB:(h + 1) * TPB].rearrange("p q n -> p (q n)"), TR[h][:]).then_inc(hiddenT_ok, 1)

            def sorted_in(t, p):
                act.wait_ge(xs_mm, t + 1)
                nc.scalar.copy(xin[:, p].rearrange("p k n -> p (k n)"), PX[:, 0:D]).then_inc(xin_ok, 1)

            def free_ys(g, u, stores, adds):
                if stores is not None:
                    act.wait_ge(stored[u], stores)
                if adds is not None:
                    act.wait_ge(added, adds)

            def iteration(g, u, phase, silu_next=True, sort=None, fetch="shared", stores=None, adds=None):
                transposed(g)
                if silu_next:
                    silu(g + 1, (u + 1) % 2)
                if fetch == "shared":
                    act.wait_ge(up_mm, (g + 1) * HALVES)
                    shared_rows(g + 2, u)
                elif fetch == "sorted":
                    act.wait_ge(up_mm, (g + 1) * HALVES)
                    sorted_in(g + (2 - TILES), u % 2)
                if sort is not None:
                    for v in range(2):
                        t, s, again = sort
                        act.wait_ge(row_mm, t + (v + 1))
                        if again is not None:
                            act.wait_ge(sorted_ok[s + v], again)
                        nc.scalar.copy(hr[:, s + v, 0, 0:D], PX[:, 0:D]).then_inc(row_ok, 1)
                act.wait_ge(down_mm, g + 1)
                free_ys(g, u, stores, adds)
                if phase == "shared":
                    nc.scalar.copy(ys[:, u], PY[:, 0:D]).then_inc(y_ok, 1)
                else:
                    nc.scalar.mul(ys[:, u], PY[:, 0:D], xs[:, u, D + 1:D + 2]).then_inc(y_ok, 1)

            silu(0, 0)
            for g in range(RING):
                iteration(g, g, "shared")
            for g in range(SORT_FROM, SORT_FROM + SORT_TILES):
                t = 2 * (g - SORT_FROM)
                u = g % RING
                iteration(g, u, "shared", sort=(t, t % RING, None if t < RING else 16 * TOP * (t // RING)),
                          stores=16 * (g // RING))
            for g in range(SORT_FROM + SORT_TILES, TILES):
                u = g % RING
                iteration(g, u, "shared", fetch="shared" if g + 2 < TILES else "sorted", stores=16 * (g // RING))
            for u in range(RING):
                iteration(TILES + u, u, "sorted", fetch="sorted", stores=16 * (TILES // RING))
            with act.Fori(1, SLOT_TILES // RING) as i:
                for u in range(RING):
                    iteration(i * RING + (TILES + u), u, "sorted", fetch="sorted", adds=i * (16 * RING) + 16 * (u + 1 - RING))
            for t in range(SLOT_TILES // RING * RING, SLOT_TILES):
                iteration(TILES + t, t % RING, "sorted", silu_next=t + 1 < SLOT_TILES,
                          fetch="sorted" if t + 2 < SLOT_TILES else None, adds=16 * (t - RING + 1))

        @block.tensor
        def _(pe):
            pe.wait_ge(wx_in, 16)
            for k in range(K):
                pe.wait_ge(x_in[k], 16)
            for n in range(NTOK // BANK):
                for m in range(K):
                    if n >= 2:
                        pe.wait_ge(xproj_ok, (n - 2) * K + m + 1)
                    for k in range(K):
                        last = nc.tensor.matmul(Z[n % 2][m][:], wx_sb[:, k, m * P:(m + 1) * P],
                                                xT[:, k, n * BANK:(n + 1) * BANK], start=k == 0, stop=k == K - 1)
                    last.then_inc(xproj_mm, 1)
            pe.wait_ge(identity_ok, 3)
            pe.wait_ge(wh_in, 16)
            pe.wait_ge(h0_in, 16)
            pe.wait_ge(xproj_ok, K * NTOK // BANK)

            def inject(p, j):
                for m in range(K):
                    nc.tensor.matmul(Z[p][m][:, 0:COLS], identity[:], xproj[:, m, bass.ds(j * COLS, COLS)],
                                     start=True, stop=False)

            def pair(z, h, r, i, first, final):
                for u in range(2):
                    for k in range(K):
                        if not (first and u == 0):
                            pe.wait_ge(h[k], i * 2 + (r * L + u))
                        for m in range(K):
                            last = nc.tensor.matmul(Z[u][m][:, 0:COLS], wh_sb[:, k, m * P:(m + 1) * P], column(k, i * 2 + u),
                                                    start=False, stop=k == K - 1)
                            if k == K - 1:
                                last.then_inc(z[m], 1)
                    if not (final and u == 1):
                        inject(1 - u, i * 2 + u + 1)

            def round_(z, h, start, r):
                pe.wait_ge(start, r + 1)
                inject(0, 0)
                pair(z, h, r, 0, True, False)
                with pe.Fori(1, L // 2 - 1) as i:
                    pair(z, h, r, i, False, False)
                pair(z, h, r, L // 2 - 1, False, True)

            for r in range(SPECULATIVE_ROUNDS):
                round_(z_mm, h_ok, start_ok, r)
            pe.wait_ge(drift_counted, 1)
            pe.wait_ge(consts, 6)
            nc.tensor.matmul(PY[:, 0:1], ones[:], same_count[:], start=True, stop=True).then_inc(drift_summed, 1)
            pe.wait_ge(drift_known, 1)
            same = pe.value_load(same_count_u[0:1, 0:1], min_val=0, max_val=EXPECTED_SAME)
            with pe.If(same != EXPECTED_SAME):
                with pe.Fori(0, GENERAL_ROUNDS) as r:
                    round_(z_mm_general, h_ok_general, start_ok_general, r)
                for k in range(K):
                    pe.wait_ge(h_ok_general[k], GENERAL_ROUNDS * L)
            for k in range(K):
                pe.wait_ge(h_ok[k], SPECULATIVE_ROUNDS * L)

            pe.wait_ge(gate_in, 16)
            for t in range(TILES):
                for k in range(K):
                    last = nc.tensor.matmul(PX[:, t * E:(t + 1) * E], states[:, k, t + 1], gate_sb[:, k],
                                            start=k == 0, stop=k == K - 1)
            last.then_inc(logits_mm, 1)
            pe.wait_ge(logits_mm, 1)
            pe.sem_inc(recurrence_over, 1)

            def up(g, p, e, first=False):
                pe.wait_ge(xin_ok, g + 1)
                if not first:
                    pe.wait_ge(hidden_ok, (g - 1) * HALVES)
                for h in range(HALVES):
                    for k in range(K):
                        last = nc.tensor.matmul(Z[p][h][:], xin[:, p, k], weight(e, k * HID + h * BANK, BANK),
                                                start=k == 0, stop=k == K - 1)
                    last.then_inc(up_mm, 1)

            def turn(g, first=False):
                for h in range(HALVES):
                    pe.wait_ge(hidden_ok, g * HALVES + (h + 1))
                    if not first:
                        pe.wait_ge(hiddenT_ok, (g - 1) * HALVES + (h + 1))
                    for q in range(TPB):
                        last = nc.tensor.transpose(TR[h][:, q * P:(q + 1) * P],
                                                   hidden[:, (h * TPB + q) * P:(h * TPB + q + 1) * P], identity[:])
                    last.then_inc(tr_mm, 1)

            def down(g, e, first=False):
                if not first:
                    pe.wait_ge(y_ok, g)
                for q in range(Q):
                    if q % TPB == 0:
                        pe.wait_ge(hiddenT_ok, g * HALVES + (q // TPB + 1))
                    last = nc.tensor.matmul(PY[:, 0:D], hiddenT[:, q], weight(e, K * HID + q * D, D),
                                            start=q == 0, stop=q == Q - 1)
                last.then_inc(down_mm, 1)

            def sorted_columns(t, u, n):
                pe.wait_ge(xs_in[u], n)
                pe.wait_ge(xin_ok, t + (TILES))
                for k in range(K):
                    last = nc.tensor.transpose(PX[:, k * P:(k + 1) * P], xs[:, u, k * P:(k + 1) * P], identity[:])
                last.then_inc(xs_mm, 1)

            def rows(t):
                if t:
                    pe.wait_ge(row_ok, t)
                for k in range(K):
                    last = nc.tensor.transpose(PX[:, k * P:(k + 1) * P], states[:, k, t + 1], identity[:])
                last.then_inc(row_mm, 1)

            pe.wait_ge(w_in[E], 16)
            up(0, 0, E, first=True)
            turn(0, first=True)
            up(1, 1, E, first=True)
            pe.wait_ge(picked_ok, 1)
            for n, m in enumerate((before, ones)):
                last = nc.tensor.matmul(PX[:, (n + 1) * P:(n + 2) * P], m[:], picked.rearrange("p t e -> p (t e)"),
                                        start=True, stop=True)
            last.then_inc(prefix_mm, 1)
            down(0, E, first=True)
            for g in range(1, RING):
                turn(g)
                up(g + 1, (g + 1) % 2, E)
                down(g, E)
            pe.wait_ge(prefix_read, 1)
            for g in range(SORT_FROM, SORT_FROM + SORT_TILES):
                turn(g)
                up(g + 1, (g + 1) % 2, E)
                for v in range(2):
                    rows(2 * (g - SORT_FROM) + v)
                down(g, E)
            for e in range(E):
                pe.wait_ge(w_in[e], 16)
            pe.wait_ge(routed, 1)
            pe.wait_ge(row_ok, TILES)

            def expert(t):
                return pe.value_load(expert_u[0:1, bass.ds(t, 1)], min_val=0, max_val=E - 1)

            for g in range(SORT_FROM + SORT_TILES, TILES - 2):
                turn(g)
                up(g + 1, (g + 1) % 2, E)
                down(g, E)
            turn(TILES - 2)
            up(TILES - 1, 1, E)
            sorted_columns(0, 0, 16)
            down(TILES - 2, E)
            turn(TILES - 1)
            now = expert(0)
            up(TILES, 0, now)
            sorted_columns(1, 1, 16)
            down(TILES - 1, E)

            def iteration(t, u, n_in, up_next=True, fetch=True):
                turn(TILES + t)
                if up_next:
                    up(TILES + t + 1, (u + 1) % 2, expert(t + 1))
                if fetch:
                    sorted_columns(t + 2, (u + 2) % RING, n_in)
                down(TILES + t, expert(t))

            with pe.Fori(0, SLOT_TILES // RING) as i:
                for u in range(RING):
                    iteration(i * RING + u, u, i * 16 + 16 * (1 + (u + 2) // RING))
            for t in range(SLOT_TILES // RING * RING, SLOT_TILES):
                iteration(t, t % RING, 16 * ((t + 2) // RING + 1), up_next=t + 1 < SLOT_TILES, fetch=t + 2 < SLOT_TILES)


def kernel(**inputs):
    import numpy as _np
    import concourse.bacc as _bacc
    from concourse import mybir as _mybir
    from concourse.bass_utils import run_bass_kernel_spmd as _run

    a = {n: _np.asarray(v) for n, v in inputs.items()}
    x = a["x"].reshape(B, C, L, D)
    w1 = _np.concatenate([a["L0_ffn_experts_w1"], a["L0_ffn_shared_w1"][None]])
    w2 = _np.concatenate([a["L0_ffn_experts_w2"], a["L0_ffn_shared_w2"][None]])
    w1 = w1.reshape(E + 1, HID, K, P).transpose(0, 3, 2, 1).reshape(E + 1, P, K * HID)
    w2 = w2.reshape(E + 1, D, Q, P).transpose(0, 3, 2, 1).reshape(E + 1, P, Q * D)
    laid = {
        "x_cols": x.transpose(3, 2, 1, 0).reshape(K, P, NTOK),
        "x_rows": x.transpose(2, 1, 0, 3).reshape(NTOK, D),
        "h0_cols": a["cond_1024"].reshape(B, K, P).transpose(2, 1, 0),
        "wx": a["L0_cond_Wx"].reshape(K, P, D).transpose(1, 0, 2),
        "wh": a["L0_cond_Wh"].reshape(K, P, D).transpose(1, 0, 2),
        "bias": a["L0_cond_b"].reshape(K, P).T,
        "weights": _np.concatenate([w1, w2], axis=2),
        "gate_cols": a["L0_ffn_gate_w"].reshape(E, K, P).transpose(2, 1, 0),
    }
    nc = _bacc.Bacc("TRN2", target_bir_lowering=False, num_devices=1)
    arrays, args = {}, []
    for name, v in laid.items():
        arrays[name] = _np.ascontiguousarray(v)
        args.append(nc.dram_tensor(name, v.shape, _mybir.dt.from_np(v.dtype), kind="ExternalInput").ap())
    rows = NTOK + P
    args.append(nc.dram_tensor("out", (rows, D), F32, kind="ExternalOutput").ap())
    build(nc, *args)
    r = _run(nc, [arrays], core_ids=[0])
    got = r.results[0]["out"][:NTOK]
    return got.reshape(L, C, B, D).transpose(2, 1, 0, 3).reshape(B, T, D)
```

```python
from contextlib import ExitStack

import numpy as np

import concourse.bass as bass
from concourse import mybir

F32 = mybir.dt.float32
F16 = mybir.dt.float16
BF16 = mybir.dt.bfloat16
U32 = mybir.dt.uint32
ALU = mybir.AluOpType
ACT = mybir.ActivationFunctionType
AX = mybir.AxisListType

P = 128
B, T, D = 2, 1024, 256
HID = 1024
E = 8
SHARED = 0
TOP = 2
K = D // P
Q = HID // P
NTOK = B * T

C = P // B
L = T // C
COLS = C * B
SPECULATIVE_ROUNDS = 3
TOLERANCE = 2.0 ** -18
EXPECTED_SAME = P * K * (COLS - B)

TILES = NTOK // P
SLOT_TILES = (TOP * NTOK + E * (P - 1)) // P
COMMON_TILES = SLOT_TILES // 4 * 4 + 1
ALL_TILES = TILES + SLOT_TILES
ROW = D + 2
BANK = 512
HALVES = HID // BANK
TPB = BANK // P
WCOLS = K * HID + Q * D
MATRIX = WCOLS // 2
CHUNK = BANK
CHUNKS = WCOLS // CHUNK
FFNS = E + 1

EXPONENT = 14
STATE_SCALE = float(2 ** EXPONENT)
LEAST_MAX = 2.0 ** -40
EXPONENT_MASK = 0x7F800000
SCALE_BITS = float((EXPONENT + 2 * 127) << 23)
UP_UNSCALE = 2.0 ** (-2 * EXPONENT)
HIDDEN_SCALE = 1.0 / D
DOWN_UNSCALE = D * 2.0 ** (-2 * EXPONENT)
RING = 4
SORT_FROM = RING
SORT_TILES = TILES // 2
EARLY_CHUNKS = 4 * CHUNKS + 4
BOUND_BATCHES = ((0, 3), (3, 6), (6, 9))


def build(nc, x_cols, x_rows, h0_cols, wx, wh, bias, weights, gate_cols, out):
    ctx = ExitStack()
    with ctx:
        def sb(name, shape, dt=F32):
            return ctx.enter_context(nc.sbuf_tensor(name, shape, dt))

        def sem(name):
            return ctx.enter_context(nc.semaphore(name))

        sorted_rows = nc.dram_tensor("sorted_rows", [SLOT_TILES * P, ROW], F32).ap()

        w_slots = sb("w_slots", [P, FFNS * CHUNKS + 1, CHUNK])
        w_split = w_slots[:].rearrange("p s c -> p (s c)").bitcast(F16)
        bound = sb("bound", [P, FFNS, 2])
        bound_all = sb("bound_all", [P, FFNS, 2])
        w_pow = sb("w_pow", [P, FFNS, 2])
        w_scale = sb("w_scale", [P, FFNS, 2])
        ffn_scales = sb("ffn_scales", [P, 3, FFNS])
        tile_scales = sb("tile_scales", [P, ALL_TILES, 3])
        states = sb("states", [P, K, L + 1, COLS])
        space = sb("space", [P, 2 * K * NTOK])
        xT = space[:, 0:K * NTOK].rearrange("p (k n) -> p k n", k=K)
        xproj = space[:, K * NTOK:2 * K * NTOK].rearrange("p (k n) -> p k n", k=K)
        recurrence_w = sb("recurrence_w", [P, 2, K, D])
        wx_sb, wh_sb = recurrence_w[:, 0], recurrence_w[:, 1]
        magnitudes = recurrence_w[:].rearrange("p w k n -> p (w k n)").bitcast(BF16)
        bias_sb = sb("bias_sb", [P, K])
        gate_sb = sb("gate_sb", [P, K, E])
        identity = sb("identity", [P, P])
        before = sb("before", [P, P])
        ones = sb("ones", [P, P])
        pad_row = sb("pad_row", [P, ROW])
        iota_e = sb("iota_e", [P, E])
        iota_full = sb("iota_full", [P, TILES])
        iota_tile = sb("iota_tile", [P, SLOT_TILES])
        token_no = sb("token_no", [P, TILES])
        same_count = sb("same_count", [P, 1])
        same_count_u = sb("same_count_u", [P, 1], U32)
        x_hi = sb("x_hi", [P, 2, K, P], F16)
        x_lo = sb("x_lo", [P, 2, K, P], F16)

        at = [0]

        def carve(*shape):
            n = int(np.prod(shape))
            v = space[:, at[0]:at[0] + n]
            at[0] += n
            assert at[0] <= 2 * K * NTOK
            if len(shape) == 1:
                return v
            if len(shape) == 2:
                return v.rearrange("p (a b) -> p a b", a=shape[0])
            return v.rearrange("p (a b c) -> p a b c", a=shape[0], b=shape[1])

        hr = carve(RING, TOP, ROW)
        hidden = carve(HID)
        hiddenT = carve(Q * P).bitcast(F16).rearrange("p (s q n) -> p s q n", s=2, q=Q)
        hT_hi, hT_lo = hiddenT[:, 0], hiddenT[:, 1]
        ys = carve(RING, D)
        x_res = carve(2, D)
        slots_u = carve(TILES, TOP).bitcast(U32)
        meta = carve(TILES, TOP, 2)
        expert_u = carve(SLOT_TILES).bitcast(U32)
        slot_idx = carve(RING, TOP).bitcast(U32)
        token_idx = carve(RING).bitcast(U32)
        used_u = carve(1).bitcast(U32)
        y_scale = carve(RING)
        n_drift = K * (COLS - B)
        drift = hidden[:, 0:n_drift].rearrange("p (k n) -> p k n", k=K)
        drift_ok = hidden[:, n_drift:2 * n_drift].rearrange("p (k n) -> p k n", k=K)
        routing_at = at[0]
        xs = carve(RING, ROW)
        at[0] = routing_at
        logits = carve(TILES, E)
        best = carve(TILES, E)
        best_at = carve(TILES, E).bitcast(U32)
        chosen = carve(TOP, TILES)
        gap = carve(TILES)
        exp_gap = carve(TILES)
        denom = carve(TILES)
        onehot = carve(TOP, TILES, E)
        picked = carve(TILES, E)
        earlier = carve(E, TILES)
        per_tile = carve(E, TILES)
        running = carve(E, TILES)
        restart = carve(E, TILES)
        slot_of = carve(E, TILES)
        masked = carve(TOP * TILES, E)
        filled = carve(E, TILES)
        tiles_of = carve(E)
        tiles_upto = carve(E)
        base = carve(E)
        slots = carve(TOP, TILES)
        ended = carve(SLOT_TILES, E)
        expert_of = carve(SLOT_TILES)
        is_expert = ended
        scale_parts = space[:, routing_at:routing_at + SLOT_TILES * E].rearrange("p (t e) -> p t e", e=E)

        Z = [[ctx.enter_context(nc.psum_tensor(f"z{p}{m}", [P, BANK], F32)) for m in range(K)] for p in range(2)]
        TR = [ctx.enter_context(nc.psum_tensor(f"tr{h}", [P, BANK], F32)) for h in range(HALVES)]
        PY = ctx.enter_context(nc.psum_tensor("py", [P, BANK], F32))
        PX = ctx.enter_context(nc.psum_tensor("px", [P, BANK], F32))

        wx_in, wh_in, x_in = sem("wx_in"), sem("wh_in"), [sem(f"x_in{n}") for n in range(NTOK // BANK)]
        bias_in, h0_in, gate_in = sem("bias_in"), sem("h0_in"), sem("gate_in")
        w_in = [sem(f"w_in{f}") for f in range(FFNS)]
        bound_ok = [sem(f"bound_ok{n}") for n in range(len(BOUND_BATCHES))]
        bound_all_ok, split_ok = sem("bound_all_ok"), sem("split_ok")
        x_res_in = [sem(f"x_res_in{u}") for u in range(2)]
        xs_in = [sem(f"xs_in{u}") for u in range(RING)]
        consts = sem("consts")
        identity_ok, pad_ok = sem("identity_ok"), sem("pad_ok")
        xproj_mm, xproj_ok = sem("xproj_mm"), sem("xproj_ok")
        start_ok = sem("start_ok")
        z_mm = [sem(f"z_mm{m}") for m in range(K)]
        h_ok = [sem(f"h_ok{k}") for k in range(K)]
        start_ok_general = sem("start_ok_general")
        z_mm_general = [sem(f"z_mm_general{m}") for m in range(K)]
        h_ok_general = [sem(f"h_ok_general{k}") for k in range(K)]
        check_chain, drift_counted, drift_summed, drift_known = sem("check_chain"), sem("drift_counted"), sem("drift_summed"), sem("drift_known")
        recurrence_over = sem("recurrence_over")
        tiles_ok = sem("tiles_ok")
        logits_mm, gap_ok, exp_ok, picked_ok, prefix_mm, prefix_read, routed = (
            sem(n) for n in "logits_mm gap_ok exp_ok picked_ok prefix_mm prefix_read routed".split())
        chain = sem("chain")
        x_hi_ok, x_lo_ok, up_mm, hidden_ok, tr_mm, h_hi_ok, h_lo_ok, down_mm, y_ok = (
            sem(n) for n in "x_hi_ok x_lo_ok up_mm hidden_ok tr_mm h_hi_ok h_lo_ok down_mm y_ok".split())
        row_mm, row_ok, row_copied = sem("row_mm"), sem("row_ok"), sem("row_copied")
        sorted_ok = [sem(f"sorted_ok{u}") for u in range(RING)]
        xs_mm, idx_ok = sem("xs_mm"), sem("idx_ok")
        summed, stored = sem("summed"), [sem(f"stored{u}") for u in range(RING)]
        added = sem("added")
        padded, padded_out = sem("padded"), sem("padded_out")
        pool_waited, sp_waited, act_waited = sem("pool_waited"), sem("sp_waited"), sem("act_waited")
        block = ctx.enter_context(nc.Block())

        GENERAL_ROUNDS = C - SPECULATIVE_ROUNDS

        def column(k, j):
            return states[:, k, bass.ds(j, 1), :].rearrange("p a n -> p (a n)")

        def weight(f, at, n, part):
            c, start = divmod(at, CHUNK)
            return w_split[:, bass.ds(f * (2 * WCOLS) + (2 * c + part) * CHUNK + start, n)]

        @block.sync
        def _(sp):
            sp.dma_start(wx_sb, wx).then_inc(wx_in, 16)
            for n in range(NTOK // BANK):
                sp.dma_start(xT[:, :, n * BANK:(n + 1) * BANK], x_cols[n]).then_inc(x_in[n], 16)
                if n == 0:
                    sp.dma_start(bias_sb[:], bias).then_inc(bias_in, 16)
            sp.dma_start(wh_sb, wh).then_inc(wh_in, 16)
            sp.dma_start(states[:, :, 0, 0:B], h0_cols).then_inc(h0_in, 16)
            sp.dma_start(gate_sb[:], gate_cols).then_inc(gate_in, 16)
            for f in range(FFNS):
                sp.dma_start(w_slots[:, f * CHUNKS + 1:(f + 1) * CHUNKS + 1].rearrange("p s c -> p (s c)"),
                             weights[f]).then_inc(w_in[f], 16)
            sp.wait_ge(pad_ok, 3)
            sp.dma_start(sorted_rows.rearrange("(t p) r -> p t r", p=P),
                         pad_row[:].unsqueeze(1).broadcast_to([P, SLOT_TILES, ROW])).then_inc(padded, 16)
            sp.dma_start(out[NTOK:NTOK + P, :], pad_row[:, 0:D]).then_inc(padded_out, 16)
            sp.wait_ge(recurrence_over, 1)
            x_tiles = x_rows.rearrange("(t p) d -> t p d", p=P)
            out_tiles = out.rearrange("(t p) d -> t p d", p=P)

            def tile_of(dram, t):
                return dram[bass.ds(t, 1), :, :].rearrange("a p d -> (a p) d")

            for g in range(2):
                sp.dma_start(x_res[:, g], x_tiles[g]).then_inc(x_res_in[g], 16)

            def store(g, u, more):
                sp.wait_ge(summed, g + 1)
                sp.dma_start(tile_of(out_tiles, g), ys[:, u]).then_inc(stored[u], 16)
                if more:
                    sp.dma_start(x_res[:, u % 2], tile_of(x_tiles, g + 2)).then_inc(x_res_in[u % 2], 16)

            with sp.Fori(0, TILES // RING - 1) as i:
                for u in range(RING):
                    store(i * RING + u, u, True)
            sorted_tiles = sorted_rows.rearrange("(t p) r -> t p r", p=P)

            def load(t, u, refill):
                if refill:
                    sp.wait_ge(xs_mm, t - RING + 1)
                    sp.sem_inc(sp_waited, 1)
                    sp.wait_ge(idx_ok, t - RING + 1)
                sp.dma_start(xs[:, u], tile_of(sorted_tiles, t)).then_inc(xs_in[u], 16)

            sp.wait_ge(tiles_ok, 1)
            for u in range(RING):
                sp.wait_ge(sorted_ok[u], 16 * TOP * TILES // RING)
            for t in range(RING):
                load(t, t, False)
            for u in range(RING):
                store(TILES - RING + u, u, u < RING - 2)
            with sp.Fori(1, SLOT_TILES // RING) as i:
                for u in range(RING):
                    load(i * RING + u, u, True)
            for t in range(SLOT_TILES // RING * RING, SLOT_TILES):
                load(t, t % RING, True)
            for t in range(COMMON_TILES, SLOT_TILES):
                sp.wait_ge(xs_in[t % RING], 16 * (t // RING + 1))

        @block.gpsimd
        def _(pool):
            nc.gpsimd.memset(identity[:], 0.0).then_inc(identity_ok, 1)
            nc.gpsimd.memset(before[:], 1.0).then_inc(identity_ok, 1)
            nc.gpsimd.memset(pad_row[:], 0.0).then_inc(pad_ok, 1)
            nc.gpsimd.memset(ones[:], 1.0).then_inc(consts, 1)
            pool.wait_ge(identity_ok, 2)
            nc.gpsimd.affine_select(out=identity[:], in_=identity[:], compare_op=ALU.not_equal, fill=1.0,
                                    base=0, pattern=[[-1, P]], channel_multiplier=1).then_inc(identity_ok, 1)
            nc.gpsimd.affine_select(out=before[:], in_=before[:], compare_op=ALU.is_gt, fill=0.0,
                                    base=0, pattern=[[1, P]], channel_multiplier=-1).then_inc(consts, 1)
            for to, pattern, start, per_partition in (
                    (iota_e[:], [[1, E]], 0, 0), (iota_full[:], [[P, TILES]], 0, 0),
                    (iota_tile[:], [[1, SLOT_TILES]], 0, 0), (token_no[:], [[P, TILES]], 0, 1)):
                nc.gpsimd.iota(to, pattern=pattern, base=start, channel_multiplier=per_partition,
                               allow_small_or_imprecise_dtypes=True).then_inc(consts, 1)
            pool.wait_ge(pad_ok, 1)
            nc.gpsimd.iota(pad_row[:, D:D + 1], pattern=[[1, 1]], base=NTOK, channel_multiplier=1,
                           allow_small_or_imprecise_dtypes=True).then_inc(pad_ok, 2)

            def waited(semaphore, value):
                pool.wait_ge(semaphore, value)
                pool.sem_inc(pool_waited, 1)

            def reduce_bounds(n, ready):
                start, end = BOUND_BATCHES[n]
                pool.wait_ge(bound_ok[n], ready)
                nc.gpsimd.partition_all_reduce(bound_all[:, start:end].rearrange("p f m -> p (f m)"),
                                               bound[:, start:end].rearrange("p f m -> p (f m)"),
                                               P, bass.bass_isa.ReduceOp.max).then_inc(bound_all_ok, 1)
            reduce_bounds(0, 1)
            reduce_bounds(1, 1)
            pool.wait_ge(routed, 1)

            def sort(t, u):
                waited(row_ok, t + 1)
                nc.gpsimd.tensor_copy(hr[:, u, :, D:ROW], meta[:, bass.ds(t, 1)].rearrange("p a k c -> p (a k) c")).then_inc(row_copied, 1)
                nc.gpsimd.tensor_copy(slot_idx[:, u], slots_u[:, bass.ds(t, 1)].rearrange("p a k -> p (a k)")).then_inc(row_copied, 1)
                waited(row_copied, t * 2 + 2)
                for k in range(TOP):
                    nc.gpsimd.indirect_dma_start(
                        out=sorted_rows, out_offset=bass.IndirectOffsetOnAxis(slot_idx[:, u, k:k + 1], 0),
                        in_=hr[:, u, k], in_offset=None).then_inc(sorted_ok[u], 16)

            pool.wait_ge(padded, 16)
            for t in range(RING):
                sort(t, t)
            reduce_bounds(2, 2 * (BOUND_BATCHES[2][1] - BOUND_BATCHES[2][0]))
            with pool.Fori(1, TILES // RING) as i:
                for u in range(RING):
                    waited(sorted_ok[u], i * (16 * TOP))
                    sort(i * RING + u, u)

            pool.wait_ge(tiles_ok, 1)
            used = pool.value_load(used_u[0:1, 0:1], min_val=1, max_val=SLOT_TILES)

            def add(t, u):
                waited(idx_ok, t + 1)
                waited(y_ok, t + (TILES + 1))
                nc.gpsimd.indirect_dma_start(
                    out=out, out_offset=bass.IndirectOffsetOnAxis(token_idx[:, u:u + 1], 0),
                    in_=ys[:, u], in_offset=None, compute_op=ALU.add).then_inc(added, 16)
                waited(added, t * 16 + 16)

            pool.wait_ge(padded_out, 16)
            for u in range(RING):
                pool.wait_ge(stored[u], 16 * TILES // RING)
            with pool.Fori(0, SLOT_TILES // RING) as i:
                for u in range(RING):
                    add(i * RING + u, u)
            for t in range(SLOT_TILES // RING * RING, COMMON_TILES):
                add(t, t % RING)
            with pool.If(used > COMMON_TILES):
                for t in range(COMMON_TILES, SLOT_TILES):
                    add(t, t % RING)

        @block.vector
        def _(dve):
            links = [0]

            def link(instruction):
                links[0] += 1
                instruction.then_inc(chain, 1)
                dve.wait_ge(chain, links[0])

            nc.vector.memset(states[:, :, 0, B:COLS], 0.0).then_inc(start_ok, 1)

            def next_start(h, count, started):
                for k in range(K):
                    dve.wait_ge(h[k], count)
                nc.vector.tensor_copy(states[:, :, 0, B:COLS], states[:, :, L, 0:COLS - B]).then_inc(started, 1)

            def find_largest(f):
                dve.wait_ge(w_in[f], 16)
                raw = w_slots[:, f * CHUNKS + 1:(f + 1) * CHUNKS + 1].rearrange("p (m s) c -> p m (s c)", m=2)
                return nc.vector.tensor_reduce(bound[:, f], raw, AX.X, ALU.max, apply_absolute_value=True)

            def find_scales(n):
                start, end = BOUND_BATCHES[n]
                dve.wait_ge(bound_all_ok, n + 1)
                flat = lambda v: v[:, start:end].rearrange("p f m -> p (f m)")
                link(nc.vector.tensor_scalar_max(flat(bound), flat(bound_all), LEAST_MAX))
                link(nc.vector.tensor_scalar(flat(w_pow).bitcast(U32), flat(bound).bitcast(U32),
                                             EXPONENT_MASK, None, ALU.bitwise_and))
                link(nc.vector.tensor_scalar(flat(w_scale).bitcast(U32), flat(w_pow).bitcast(U32),
                                             -1.0, SCALE_BITS, ALU.mult, ALU.add))
                nc.vector.tensor_scalar_mul(ffn_scales[:, 0, start:end], w_pow[:, start:end, 0], UP_UNSCALE)
                nc.vector.tensor_scalar_mul(ffn_scales[:, 1, start:end], w_scale[:, start:end, 0], HIDDEN_SCALE)
                link(nc.vector.scalar_tensor_tensor(ffn_scales[:, 2, start:end], w_pow[:, start:end, 0],
                                                    DOWN_UNSCALE, w_pow[:, start:end, 1], ALU.mult, ALU.mult))

            def split(c):
                f, m = c // CHUNKS, c % CHUNKS // (CHUNKS // 2)
                high, low = (w_split[:, (2 * c + part) * CHUNK:(2 * c + part + 1) * CHUNK] for part in range(2))
                scale = w_scale[:, f, m:m + 1]
                if c:
                    dve.wait_ge(split_ok, c)
                link(nc.vector.tensor_scalar(high, w_slots[:, c + 1], scale, None, ALU.mult))
                nc.vector.scalar_tensor_tensor(low, w_slots[:, c + 1], scale, high, ALU.mult, ALU.subtract).then_inc(split_ok, 1)

            for f in range(0, 3):
                last = find_largest(f)
            last.then_inc(bound_ok[0], 1)
            find_scales(0)
            link(nc.vector.tensor_copy(tile_scales[:, 0:TILES].rearrange("p t s -> p s t"),
                                       ffn_scales[:, :, 0:1].broadcast_to([P, 3, TILES])))
            for c in range(0, CHUNKS):
                split(c)
            next_start(h_ok, L, start_ok)
            for f in range(3, 6):
                last = find_largest(f)
            last.then_inc(bound_ok[1], 1)
            for c in range(CHUNKS, 2 * CHUNKS):
                split(c)
            next_start(h_ok, 2 * L, start_ok)
            find_scales(1)
            for c in range(2 * CHUNKS, EARLY_CHUNKS):
                split(c)

            for k in range(K):
                dve.wait_ge(h_ok[k], SPECULATIVE_ROUNDS * L)
            link(nc.vector.tensor_sub(drift, states[:, :, L, 0:COLS - B], states[:, :, 0, B:COLS]))
            link(nc.vector.tensor_mul(drift_ok, drift, drift))
            link(nc.vector.tensor_scalar(drift, drift_ok, TOLERANCE ** 2, None, ALU.is_le))
            nc.vector.tensor_reduce(same_count[:], drift, AX.XY, ALU.add).then_inc(drift_counted, 1)
            dve.wait_ge(drift_summed, 1)
            nc.vector.tensor_copy(same_count_u[:], PY[:, 0:1]).then_inc(drift_known, 1)
            dve.wait_ge(drift_known, 1)
            same = dve.value_load(same_count_u[0:1, 0:1], min_val=0, max_val=EXPECTED_SAME)
            with dve.If(same != EXPECTED_SAME):
                next_start(h_ok, SPECULATIVE_ROUNDS * L, start_ok_general)
                with dve.Fori(1, GENERAL_ROUNDS) as r:
                    next_start(h_ok_general, r * L, start_ok_general)
            dve.engine_nop()

            def states_low(g, source, p):
                dve.wait_ge(x_hi_ok, g + 1)
                nc.vector.scalar_tensor_tensor(x_lo[:, p], source, STATE_SCALE, x_hi[:, p],
                                               ALU.mult, ALU.subtract).then_inc(x_lo_ok, 1)

            def shared_states(g):
                return states[:, :, bass.ds(g + 1, 1), :].rearrange("p k a n -> p k (a n)")

            def hidden_low(g):
                for h in range(HALVES):
                    dve.wait_ge(h_hi_ok, g * HALVES + (h + 1))
                    part = slice(h * TPB, (h + 1) * TPB)
                    nc.vector.scalar_tensor_tensor(
                        hT_lo[:, part].rearrange("p q n -> p (q n)"), TR[h][:],
                        tile_scales[:, bass.ds(g, 1), 1:2].rearrange("p a n -> p (a n)"),
                        hT_hi[:, part].rearrange("p q n -> p (q n)"), ALU.mult, ALU.subtract).then_inc(h_lo_ok, 1)

            def residual(g):
                u = g % RING
                dve.wait_ge(x_res_in[u % 2], 16 * (g // 2 + 1))
                dve.wait_ge(y_ok, g + 1)
                nc.vector.tensor_add(ys[:, u], ys[:, u], x_res[:, u % 2]).then_inc(summed, 1)

            def index(t, u, n, again):
                dve.wait_ge(xs_in[u], n)
                if again:
                    dve.wait_ge(added, (t - RING + 1) * 16)
                nc.vector.tensor_copy(token_idx[:, u:u + 1], xs[:, u, D:D + 1])
                nc.vector.tensor_mul(y_scale[:, u:u + 1], xs[:, u, D + 1:D + 2],
                                     tile_scales[:, bass.ds(t + TILES, 1), 2:3].rearrange("p a n -> p (a n)")).then_inc(idx_ok, 1)

            def route_gap():
                dve.wait_ge(logits_mm, 1)
                link(nc.vector.tensor_copy(logits, PX[:, 0:TILES * E].rearrange("p (t e) -> p t e", e=E)))
                for t in range(TILES):
                    last = nc.vector.max(best[:, t], logits[:, t])
                link(last)
                nc.vector.tensor_sub(gap, best[:, :, 1], best[:, :, 0]).then_inc(gap_ok, 1)

            def route_choice():
                for t in range(TILES):
                    last = nc.vector.max_index(best_at[:, t], best[:, t], logits[:, t])
                link(last)
                for k in range(TOP):
                    last = nc.vector.tensor_copy(chosen[:, k], best_at[:, :, k])
                link(last)
                dve.wait_ge(consts, 6)
                for k in range(TOP):
                    last = nc.vector.tensor_tensor(
                        onehot[:, k], chosen[:, k].unsqueeze(2).broadcast_to([P, TILES, E]),
                        iota_e[:].unsqueeze(1).broadcast_to([P, TILES, E]), ALU.is_equal)
                link(last)
                nc.vector.tensor_add(picked, onehot[:, 0], onehot[:, 1]).then_inc(picked_ok, 1)
                link(nc.vector.memset(restart, 1.0))
                link(nc.vector.memset(restart[:, :, 0:1], 0.0))

            def route_gates():
                dve.wait_ge(exp_ok, 1)
                link(nc.vector.tensor_scalar_add(denom, exp_gap, 1.0))
                link(nc.vector.reciprocal(meta[:, :, 0, 1], denom))
                nc.vector.tensor_mul(meta[:, :, 1, 1], exp_gap, meta[:, :, 0, 1])
                for k in range(TOP):
                    nc.vector.tensor_copy(meta[:, :, k, 0], token_no[:])

            def route_slots():
                dve.wait_ge(prefix_mm, 1)
                nc.vector.tensor_copy(earlier, PX[:, P:2 * P].rearrange("p (t e) -> p e t", e=E))
                prefix = nc.vector.tensor_copy(per_tile, PX[:, 2 * P:3 * P].rearrange("p (t e) -> p e t", e=E))
                prefix.then_inc(prefix_read, 1)
                dve.wait_ge(prefix_read, 1)
                flat = lambda v: v.rearrange("p e t -> p (e t)")
                link(nc.vector.tensor_tensor_scan(flat(running), flat(restart), flat(per_tile), 0.0, ALU.mult, ALU.add))
                link(nc.vector.tensor_tensor(filled, running[:, :, TILES - 1:TILES].broadcast_to([P, E, TILES]),
                                             iota_full[:].unsqueeze(1).broadcast_to([P, E, TILES]), ALU.is_gt))
                link(nc.vector.tensor_reduce(tiles_of, filled, AX.X, ALU.add))
                link(nc.vector.tensor_tensor_scan(tiles_upto, ones[:, 0:E], tiles_of, 0.0, ALU.mult, ALU.add))
                nc.vector.tensor_copy(used_u, tiles_upto[:, E - 1:E])
                nc.vector.tensor_tensor(ended, tiles_upto.unsqueeze(1).broadcast_to([P, SLOT_TILES, E]),
                                        iota_tile[:].unsqueeze(2).broadcast_to([P, SLOT_TILES, E]), ALU.is_le)
                link(nc.vector.tensor_sub(base, tiles_upto, tiles_of))
                link(nc.vector.tensor_scalar_mul(tiles_upto, base, float(P)))
                link(nc.vector.tensor_sub(slot_of, running, per_tile))
                link(nc.vector.tensor_add(slot_of, slot_of, earlier))
                link(nc.vector.tensor_add(slot_of, slot_of, tiles_upto.unsqueeze(2).broadcast_to([P, E, TILES])))
                for k in range(TOP):
                    last = nc.vector.tensor_mul(masked[:, k * TILES:(k + 1) * TILES], onehot[:, k], slot_of.rearrange("p e t -> p t e"))
                link(last)
                link(nc.vector.tensor_reduce(slots.rearrange("p k t -> p (k t)"), masked, AX.X, ALU.add))
                for k in range(TOP):
                    last = nc.vector.tensor_copy(slots_u[:, :, k], slots[:, k])
                last.then_inc(routed, 1)

            def route_tiles():
                link(nc.vector.tensor_reduce(expert_of, ended, AX.X, ALU.add))
                link(nc.vector.tensor_scalar_min(expert_of, expert_of, float(E - 1)))
                nc.vector.tensor_scalar_add(expert_u, expert_of, 1.0)
                link(nc.vector.tensor_tensor(is_expert, expert_of.unsqueeze(2).broadcast_to([P, SLOT_TILES, E]),
                                             iota_e[:].unsqueeze(1).broadcast_to([P, SLOT_TILES, E]), ALU.is_equal))
                for n in range(3):
                    link(nc.vector.tensor_mul(scale_parts, is_expert,
                                              ffn_scales[:, n, 1:FFNS].unsqueeze(1).broadcast_to([P, SLOT_TILES, E])))
                    last = nc.vector.tensor_reduce(tile_scales[:, TILES:ALL_TILES, n], scale_parts, AX.X, ALU.add)
                    if n < 2:
                        link(last)
                last.then_inc(tiles_ok, 1)

            for g in range(2):
                states_low(g, shared_states(g), g)
            split_done = [EARLY_CHUNKS]

            def split_upto(end):
                for c in range(split_done[0], end):
                    split(c)
                split_done[0] = end

            route_gap()
            route_choice()
            for g in range(TILES):
                hidden_low(g)
                if g + 2 < TILES:
                    states_low(g + 2, shared_states(g + 2), g % 2)
                else:
                    states_low(g + 2, PX[:, 0:D].rearrange("p (k n) -> p k n", k=K), g % 2)
                if g >= 1:
                    residual(g - 1)
                if g == 0:
                    route_gates()
                elif g == 1:
                    route_slots()
                elif g == 6:
                    find_scales(2)
                    route_tiles()
                elif g < TILES - 1:
                    done = g - 2 if g < 6 else g - 3
                    split_upto(EARLY_CHUNKS + -(-(FFNS * CHUNKS - EARLY_CHUNKS) * (done + 1) // (TILES - 4)))
            residual(TILES - 1)
            index(0, 0, 16, False)

            def expert(t, u, n, again, fetch=True, index_next=True):
                hidden_low(t + TILES)
                if fetch:
                    states_low(t + (TILES + 2), PX[:, 0:D].rearrange("p (k n) -> p k n", k=K), u % 2)
                if index_next:
                    index(t + 1, (u + 1) % RING, n, again)

            for t in range(RING):
                expert(t, t, 16 * ((t + 1) // RING + 1), t + 1 >= RING)
            with dve.Fori(1, SLOT_TILES // RING) as i:
                for u in range(RING):
                    expert(i * RING + u, u, i * 16 + 16 * ((u + 1) // RING + 1), True)
            for t in range(SLOT_TILES // RING * RING, COMMON_TILES):
                expert(t, t % RING, 16 * ((t + 1) // RING + 1), True, fetch=False, index_next=t + 1 < COMMON_TILES)
            used = dve.value_load(used_u[0:1, 0:1], min_val=1, max_val=SLOT_TILES)
            with dve.If(used > COMMON_TILES):
                t = COMMON_TILES
                index(t, t % RING, 16 * (t // RING + 1), True)
                states_low(t + 1 + TILES, PX[:, 0:D].rearrange("p (k n) -> p k n", k=K), (t + 1) % 2)
                for t in range(COMMON_TILES, SLOT_TILES):
                    expert(t, t % RING, 16 * ((t + 1) // RING + 1), True, fetch=False, index_next=t + 1 < SLOT_TILES)

        @block.scalar
        def _(act):
            act.wait_ge(bias_in, 16)
            for n in range(NTOK // BANK):
                for m in range(K):
                    act.wait_ge(xproj_mm, n * K + m + 1)
                    nc.scalar.activation(xproj[:, m, n * BANK:(n + 1) * BANK], Z[n % 2][m][:], ACT.Identity,
                                         bias=bias_sb[:, m:m + 1]).then_inc(xproj_ok, 1)

            def steps(z, h, r):
                with act.Fori(0, L // 2) as i:
                    for u in range(2):
                        for m in range(K):
                            act.wait_ge(z[m], i * 2 + (r * L + u + 1))
                            nc.scalar.activation(column(m, i * 2 + u + 1), Z[u][m][:, 0:COLS], ACT.Tanh).then_inc(h[m], 1)

            for r in range(SPECULATIVE_ROUNDS):
                steps(z_mm, h_ok, r)
            for k in range(K):
                act.wait_ge(h_ok[k], SPECULATIVE_ROUNDS * L)
            act.wait_ge(drift_known, 1)
            same = act.value_load(same_count_u[0:1, 0:1], min_val=0, max_val=EXPECTED_SAME)
            with act.If(same != EXPECTED_SAME):
                with act.Fori(0, GENERAL_ROUNDS) as r:
                    steps(z_mm_general, h_ok_general, r)
                for k in range(K):
                    act.wait_ge(h_ok_general[k], GENERAL_ROUNDS * L)

            def shared_rows(g, u):
                nc.scalar.mul(x_hi[:, u % 2], states[:, :, bass.ds(g + 1, 1), :].rearrange("p k a n -> p k (a n)"),
                              STATE_SCALE).then_inc(x_hi_ok, 1)

            for g in range(2):
                shared_rows(g, g)
            def find_bound(n):
                f, m = BOUND_BATCHES[2][0] + n // 2, n % 2
                act.wait_ge(w_in[f], 16)
                if n:
                    act.wait_ge(bound_ok[2], n)
                raw = w_slots[:, f * CHUNKS + 1 + m * CHUNKS // 2:f * CHUNKS + 1 + (m + 1) * CHUNKS // 2]
                nc.scalar.activation(magnitudes, raw.rearrange("p s c -> p (s c)"), ACT.Abs,
                                     accum_out=bound[:, f, m:m + 1]).then_inc(bound_ok[2], 1)

            act.wait_ge(gap_ok, 1)
            nc.scalar.activation(exp_gap, gap, ACT.Exp).then_inc(exp_ok, 1)

            def tile_scale(g, n):
                return tile_scales[:, bass.ds(g, 1), n:n + 1].rearrange("p a n -> p (a n)")

            def silu(g, p):
                for h in range(HALVES):
                    act.wait_ge(up_mm, g * HALVES + (h + 1))
                    if h == 0 and not (isinstance(g, int) and g == 0):
                        act.wait_ge(tr_mm, g * HALVES)
                    act.sem_inc(act_waited, 1)
                    nc.scalar.activation(hidden[:, h * BANK:(h + 1) * BANK], Z[p][h][:], ACT.Silu,
                                         scale=tile_scale(g, 0)).then_inc(hidden_ok, 1)

            def transposed(g):
                for h in range(HALVES):
                    act.wait_ge(tr_mm, g * HALVES + (h + 1))
                    if h == 0 and not (isinstance(g, int) and g == 0):
                        act.wait_ge(down_mm, g)
                    act.sem_inc(act_waited, 1)
                    nc.scalar.mul(hT_hi[:, h * TPB:(h + 1) * TPB].rearrange("p q n -> p (q n)"), TR[h][:],
                                  tile_scale(g, 1)).then_inc(h_hi_ok, 1)

            def sorted_in(t, p):
                act.wait_ge(xs_mm, t + 1)
                nc.scalar.mul(x_hi[:, p].rearrange("p k n -> p (k n)"), PX[:, 0:D], STATE_SCALE).then_inc(x_hi_ok, 1)

            def free_ys(g, u, stores, adds):
                if stores is not None:
                    act.wait_ge(stored[u], stores)
                if adds is not None:
                    act.wait_ge(added, adds)

            def iteration(g, u, phase, silu_next=True, sort=None, fetch="shared", stores=None, adds=None, find=None):
                def sort_row(v):
                    t, s, again = sort
                    act.wait_ge(row_mm, t + (v + 1))
                    if again is not None:
                        act.wait_ge(sorted_ok[s + v], again)
                    nc.scalar.copy(hr[:, s + v, :, 0:D],
                                   PX[:, 0:D].unsqueeze(1).broadcast_to([P, TOP, D])).then_inc(row_ok, 1)

                if sort is not None:
                    sort_row(0)
                transposed(g)
                if silu_next:
                    silu(g + 1, (u + 1) % 2)
                if fetch == "shared":
                    act.wait_ge(up_mm, (g + 1) * HALVES)
                    shared_rows(g + 2, u)
                elif fetch == "sorted":
                    act.wait_ge(up_mm, (g + 1) * HALVES)
                    sorted_in(g + (2 - TILES), u % 2)
                if sort is not None:
                    sort_row(1)
                if find is not None:
                    find_bound(find)
                act.wait_ge(down_mm, g + 1)
                free_ys(g, u, stores, adds)
                if phase == "shared":
                    nc.scalar.mul(ys[:, u], PY[:, 0:D], tile_scale(g, 2)).then_inc(y_ok, 1)
                else:
                    act.wait_ge(idx_ok, g - (TILES - 1))
                    nc.scalar.mul(ys[:, u], PY[:, 0:D], y_scale[:, u:u + 1]).then_inc(y_ok, 1)

            act.wait_ge(split_ok, 1)
            silu(0, 0)
            for g in range(RING):
                iteration(g, g, "shared", find=g)
            for g in range(SORT_FROM, SORT_FROM + SORT_TILES):
                t = 2 * (g - SORT_FROM)
                u = g % RING
                iteration(g, u, "shared", sort=(t, t % RING, None if t < RING else 16 * TOP * (t // RING)),
                          stores=16 * (g // RING), find=g if g < 2 * (BOUND_BATCHES[2][1] - BOUND_BATCHES[2][0]) else None)
            act.wait_ge(tiles_ok, 1)
            for g in range(SORT_FROM + SORT_TILES, TILES):
                u = g % RING
                iteration(g, u, "shared", fetch="shared" if g + 2 < TILES else "sorted", stores=16 * (g // RING))
            for u in range(RING):
                iteration(TILES + u, u, "sorted", fetch="sorted", stores=16 * (TILES // RING))
            with act.Fori(1, SLOT_TILES // RING) as i:
                for u in range(RING):
                    iteration(i * RING + (TILES + u), u, "sorted", fetch="sorted", adds=i * (16 * RING) + 16 * (u + 1 - RING))
            def last_iteration(t, end):
                iteration(TILES + t, t % RING, "sorted", silu_next=t + 1 < end, fetch=None, adds=16 * (t - RING + 1))

            for t in range(SLOT_TILES // RING * RING, COMMON_TILES):
                last_iteration(t, COMMON_TILES)
            used = act.value_load(used_u[0:1, 0:1], min_val=1, max_val=SLOT_TILES)
            with act.If(used > COMMON_TILES):
                sorted_in(COMMON_TILES + 1, (COMMON_TILES + 1) % 2)
                silu(TILES + COMMON_TILES, COMMON_TILES % 2)
                for t in range(COMMON_TILES, SLOT_TILES):
                    last_iteration(t, SLOT_TILES)

        @block.tensor
        def _(pe):
            pe.wait_ge(wx_in, 16)
            for n in range(NTOK // BANK):
                pe.wait_ge(x_in[n], 16)
                for m in range(K):
                    if n >= 2:
                        pe.wait_ge(xproj_ok, (n - 2) * K + m + 1)
                    for k in range(K):
                        last = nc.tensor.matmul(Z[n % 2][m][:], wx_sb[:, k, m * P:(m + 1) * P],
                                                xT[:, k, n * BANK:(n + 1) * BANK], start=k == 0, stop=k == K - 1)
                    last.then_inc(xproj_mm, 1)
            pe.wait_ge(identity_ok, 3)
            pe.wait_ge(wh_in, 16)
            pe.wait_ge(h0_in, 16)
            pe.wait_ge(xproj_ok, K * NTOK // BANK)

            def inject(p, j):
                for m in range(K):
                    nc.tensor.matmul(Z[p][m][:, 0:COLS], identity[:], xproj[:, m, bass.ds(j * COLS, COLS)],
                                     start=True, stop=False)

            def router(start, end):
                for t in range(start, end):
                    for k in range(K):
                        last = nc.tensor.matmul(PX[:, t * E:(t + 1) * E], states[:, k, t + 1], gate_sb[:, k],
                                                start=k == 0, stop=k == K - 1)
                return last

            def pair(z, h, r, i, first, final, route=False):
                for u in range(2):
                    for k in range(K):
                        if not (first and u == 0):
                            pe.wait_ge(h[k], i * 2 + (r * L + u))
                        for m in range(K):
                            last = nc.tensor.matmul(Z[u][m][:, 0:COLS], wh_sb[:, k, m * P:(m + 1) * P], column(k, i * 2 + u),
                                                    start=False, stop=k == K - 1)
                            if k == K - 1:
                                last.then_inc(z[m], 1)
                    if not (final and u == 1):
                        inject(1 - u, i * 2 + u + 1)
                    if route and i * 2 + u:
                        router(i * 2 + u - 1, i * 2 + u)

            def round_(z, h, start, r):
                pe.wait_ge(start, r + 1)
                inject(0, 0)
                pair(z, h, r, 0, True, False)
                with pe.Fori(1, L // 2 - 1) as i:
                    pair(z, h, r, i, False, False)
                pair(z, h, r, L // 2 - 1, False, True)

            for r in range(SPECULATIVE_ROUNDS - 1):
                round_(z_mm, h_ok, start_ok, r)
            pe.wait_ge(gate_in, 16)
            pe.wait_ge(start_ok, SPECULATIVE_ROUNDS)
            inject(0, 0)
            for i in range(L // 2):
                pair(z_mm, h_ok, SPECULATIVE_ROUNDS - 1, i, i == 0, i == L // 2 - 1, route=True)
            pe.wait_ge(drift_counted, 1)
            pe.wait_ge(consts, 6)
            nc.tensor.matmul(PY[:, 0:1], ones[:], same_count[:], start=True, stop=True).then_inc(drift_summed, 1)
            pe.wait_ge(drift_known, 1)
            same = pe.value_load(same_count_u[0:1, 0:1], min_val=0, max_val=EXPECTED_SAME)
            with pe.If(same != EXPECTED_SAME):
                with pe.Fori(0, GENERAL_ROUNDS) as r:
                    round_(z_mm_general, h_ok_general, start_ok_general, r)
                for k in range(K):
                    pe.wait_ge(h_ok_general[k], GENERAL_ROUNDS * L)
                router(0, TILES - 1)
            for k in range(K):
                pe.wait_ge(h_ok[k], SPECULATIVE_ROUNDS * L)
            router(TILES - 1, TILES).then_inc(logits_mm, 1)
            pe.wait_ge(logits_mm, 1)
            pe.sem_inc(recurrence_over, 1)

            def up(g, p, f, first=False):
                pe.wait_ge(x_hi_ok, g + 1)
                pe.wait_ge(x_lo_ok, g + 1)
                if not first:
                    pe.wait_ge(hidden_ok, (g - 1) * HALVES)
                for h in range(HALVES):
                    for k in range(K):
                        for x, part in ((x_hi, 0), (x_hi, 1), (x_lo, 0)):
                            last = nc.tensor.matmul(Z[p][h][:], x[:, p, k], weight(f, k * HID + h * BANK, BANK, part),
                                                    start=k == 0 and x is x_hi and part == 0,
                                                    stop=k == K - 1 and x is x_lo)
                    last.then_inc(up_mm, 1)

            def turn(g, first=False):
                for h in range(HALVES):
                    pe.wait_ge(hidden_ok, g * HALVES + (h + 1))
                    if not first:
                        pe.wait_ge(h_lo_ok, (g - 1) * HALVES + (h + 1))
                    for q in range(TPB):
                        last = nc.tensor.transpose(TR[h][:, q * P:(q + 1) * P],
                                                   hidden[:, (h * TPB + q) * P:(h * TPB + q + 1) * P], identity[:])
                    last.then_inc(tr_mm, 1)

            def down(g, f, first=False):
                if not first:
                    pe.wait_ge(y_ok, g)
                for x, ready in ((hT_hi, h_hi_ok), (hT_lo, h_lo_ok)):
                    for q in range(Q):
                        if q % TPB == 0:
                            pe.wait_ge(ready, g * HALVES + (q // TPB + 1))
                        for part in range(2 if x is hT_hi else 1):
                            last = nc.tensor.matmul(PY[:, 0:D], x[:, q], weight(f, MATRIX + q * D, D, part),
                                                    start=q == 0 and x is hT_hi and part == 0,
                                                    stop=q == Q - 1 and x is hT_lo)
                last.then_inc(down_mm, 1)

            def sorted_columns(t, u, n):
                pe.wait_ge(xs_in[u], n)
                pe.wait_ge(x_lo_ok, t + TILES)
                for k in range(K):
                    last = nc.tensor.transpose(PX[:, k * P:(k + 1) * P], xs[:, u, k * P:(k + 1) * P], identity[:])
                last.then_inc(xs_mm, 1)

            def rows(t):
                if t:
                    pe.wait_ge(row_ok, t)
                for k in range(K):
                    last = nc.tensor.transpose(PX[:, k * P:(k + 1) * P], states[:, k, t + 1], identity[:])
                last.then_inc(row_mm, 1)

            pe.wait_ge(split_ok, CHUNKS)
            up(0, 0, SHARED, first=True)
            turn(0, first=True)
            up(1, 1, SHARED, first=True)
            pe.wait_ge(picked_ok, 1)
            for n, m in enumerate((before, ones)):
                last = nc.tensor.matmul(PX[:, (n + 1) * P:(n + 2) * P], m[:], picked.rearrange("p t e -> p (t e)"),
                                        start=True, stop=True)
            last.then_inc(prefix_mm, 1)
            down(0, SHARED, first=True)
            for g in range(1, RING):
                turn(g)
                up(g + 1, (g + 1) % 2, SHARED)
                down(g, SHARED)
            pe.wait_ge(prefix_read, 1)
            for g in range(SORT_FROM, SORT_FROM + SORT_TILES):
                rows(2 * (g - SORT_FROM))
                turn(g)
                up(g + 1, (g + 1) % 2, SHARED)
                rows(2 * (g - SORT_FROM) + 1)
                down(g, SHARED)
            pe.wait_ge(tiles_ok, 1)
            pe.wait_ge(row_ok, TILES)

            def expert(t):
                return pe.value_load(expert_u[0:1, bass.ds(t, 1)], min_val=1, max_val=E)

            for g in range(SORT_FROM + SORT_TILES, TILES - 2):
                turn(g)
                up(g + 1, (g + 1) % 2, SHARED)
                down(g, SHARED)
            turn(TILES - 2)
            up(TILES - 1, 1, SHARED)
            sorted_columns(0, 0, 16)
            down(TILES - 2, SHARED)
            turn(TILES - 1)
            pe.wait_ge(split_ok, FFNS * CHUNKS)
            up(TILES, 0, expert(0))
            sorted_columns(1, 1, 16)
            down(TILES - 1, SHARED)

            def iteration(t, u, n_in, up_next=True, fetch=True):
                turn(TILES + t)
                if up_next:
                    up(TILES + t + 1, (u + 1) % 2, expert(t + 1))
                if fetch:
                    sorted_columns(t + 2, (u + 2) % RING, n_in)
                down(TILES + t, expert(t))

            with pe.Fori(0, SLOT_TILES // RING) as i:
                for u in range(RING):
                    iteration(i * RING + u, u, i * 16 + 16 * (1 + (u + 2) // RING))
            for t in range(SLOT_TILES // RING * RING, COMMON_TILES):
                iteration(t, t % RING, 0, up_next=t + 1 < COMMON_TILES, fetch=False)
            used = pe.value_load(used_u[0:1, 0:1], min_val=1, max_val=SLOT_TILES)
            with pe.If(used > COMMON_TILES):
                t = COMMON_TILES
                up(TILES + t, t % 2, expert(t))
                sorted_columns(t + 1, (t + 1) % RING, 16 * ((t + 1) // RING + 1))
                for t in range(COMMON_TILES, SLOT_TILES):
                    iteration(t, t % RING, 0, up_next=t + 1 < SLOT_TILES, fetch=False)


def kernel(**inputs):
    import numpy as _np
    import concourse.bacc as _bacc
    from concourse import mybir as _mybir
    from concourse.bass_utils import run_bass_kernel_spmd as _run

    a = {n: _np.asarray(v) for n, v in inputs.items()}
    x = a["x"].reshape(B, C, L, D)
    w1 = _np.concatenate([a["L0_ffn_shared_w1"][None], a["L0_ffn_experts_w1"]])
    w2 = _np.concatenate([a["L0_ffn_shared_w2"][None], a["L0_ffn_experts_w2"]])
    w1 = w1.reshape(E + 1, HID, K, P).transpose(0, 3, 2, 1).reshape(E + 1, P, K * HID)
    w2 = w2.reshape(E + 1, D, Q, P).transpose(0, 3, 2, 1).reshape(E + 1, P, Q * D)
    laid = {
        "x_cols": x.transpose(3, 2, 1, 0).reshape(K, P, NTOK // BANK, BANK).transpose(2, 1, 0, 3),
        "x_rows": x.transpose(2, 1, 0, 3).reshape(NTOK, D),
        "h0_cols": a["cond_1024"].reshape(B, K, P).transpose(2, 1, 0),
        "wx": a["L0_cond_Wx"].reshape(K, P, D).transpose(1, 0, 2),
        "wh": a["L0_cond_Wh"].reshape(K, P, D).transpose(1, 0, 2),
        "bias": a["L0_cond_b"].reshape(K, P).T,
        "weights": _np.concatenate([w1, w2], axis=2),
        "gate_cols": a["L0_ffn_gate_w"].reshape(E, K, P).transpose(2, 1, 0),
    }
    nc = _bacc.Bacc("TRN2", target_bir_lowering=False, num_devices=1)
    arrays, args = {}, []
    for name, v in laid.items():
        arrays[name] = _np.ascontiguousarray(v)
        args.append(nc.dram_tensor(name, v.shape, _mybir.dt.from_np(v.dtype), kind="ExternalInput").ap())
    rows = NTOK + P
    args.append(nc.dram_tensor("out", (rows, D), F32, kind="ExternalOutput").ap())
    build(nc, *args)
    r = _run(nc, [arrays], core_ids=[0])
    got = r.results[0]["out"][:NTOK]
    return got.reshape(L, C, B, D).transpose(2, 1, 0, 3).reshape(B, T, D)
```

```python
from contextlib import ExitStack

import numpy as np

import concourse.bass as bass
from concourse import mybir

F32 = mybir.dt.float32
F16 = mybir.dt.float16
BF16 = mybir.dt.bfloat16
U32 = mybir.dt.uint32
ALU = mybir.AluOpType
ACT = mybir.ActivationFunctionType
AX = mybir.AxisListType

P = 128
B, T, D = 2, 1024, 256
HID = 1024
E = 8
SHARED = 0
TOP = 2
K = D // P
Q = HID // P
NTOK = B * T

C = P // B
L = T // C
COLS = C * B
EXACT_ROUNDS = 2
SPECULATIVE_ROUNDS = 1 + EXACT_ROUNDS
MAX_F16 = 65504.0
TOLERANCE = 2.0 ** -18
EXPECTED_SAME = P * K * (COLS - B)

TILES = NTOK // P
SLOT_TILES = (TOP * NTOK + E * (P - 1)) // P
COMMON_TILES = SLOT_TILES // 4 * 4 + 1
ALL_TILES = TILES + SLOT_TILES
ROW = D + 2
BANK = 512
HALVES = HID // BANK
TPB = BANK // P
WCOLS = K * HID + Q * D
MATRIX = WCOLS // 2
CHUNK = BANK
CHUNKS = WCOLS // CHUNK
FFNS = E + 1

EXPONENT = 14
STATE_SCALE = float(2 ** EXPONENT)
LEAST_MAX = 2.0 ** -40
EXPONENT_MASK = 0x7F800000
SCALE_BITS = float((EXPONENT + 2 * 127) << 23)
UP_UNSCALE = 2.0 ** (-2 * EXPONENT)
HIDDEN_SCALE = 1.0 / D
DOWN_UNSCALE = D * 2.0 ** (-2 * EXPONENT)
RING = 4
SORT_FROM = RING
SORT_TILES = TILES // 2
EARLY_CHUNKS = 4 * CHUNKS + 6
BOUND_BATCHES = ((0, 2), (2, 3), (3, 4), (4, 5), (5, 7), (7, FFNS))
FOUND_BY_DVE = BOUND_BATCHES[0][1]
FOUND_LATE = 6
FIND_TILES = 6
FINDS = (FFNS - FOUND_LATE) * CHUNKS // FIND_TILES


def build(nc, x_cols, x_rows, h0_cols, wx, wh, bias, weights, gate_cols, out):
    ctx = ExitStack()
    with ctx:
        def sb(name, shape, dt=F32):
            return ctx.enter_context(nc.sbuf_tensor(name, shape, dt))

        def sem(name):
            return ctx.enter_context(nc.semaphore(name))

        sorted_rows = nc.dram_tensor("sorted_rows", [SLOT_TILES * P, ROW], F32).ap()

        w_slots = sb("w_slots", [P, FFNS * CHUNKS + 1, CHUNK])
        w_split = w_slots[:].rearrange("p s c -> p (s c)").bitcast(F16)
        chunk_bound = sb("chunk_bound", [P, FFNS, CHUNKS])
        chunk_bound_all = sb("chunk_bound_all", [P, FFNS, CHUNKS])
        bound = sb("bound", [P, FFNS, 2])
        magnitudes = sb("magnitudes", [P, CHUNK], BF16)
        w_pow = sb("w_pow", [P, FFNS, 2])
        w_scale = sb("w_scale", [P, FFNS, 2])
        ffn_scales = sb("ffn_scales", [P, 3, FFNS])
        tile_scales = sb("tile_scales", [P, ALL_TILES, 3])
        states = sb("states", [P, K, L + 1, COLS])
        space = sb("space", [P, 2 * K * NTOK])
        xT = space[:, 0:K * NTOK].rearrange("p (k n) -> p k n", k=K)
        xproj = space[:, K * NTOK:2 * K * NTOK].rearrange("p (k n) -> p k n", k=K)
        recurrence_w = sb("recurrence_w", [P, 2, K, D])
        wx_sb, wh_sb = recurrence_w[:, 0], recurrence_w[:, 1]
        bias_sb = sb("bias_sb", [P, K])
        gate_sb = sb("gate_sb", [P, K, E])
        identity = sb("identity", [P, P])
        before = sb("before", [P, P])
        ones = sb("ones", [P, P])
        pad_row = sb("pad_row", [P, ROW])
        iota_e = sb("iota_e", [P, E])
        iota_full = sb("iota_full", [P, TILES])
        iota_tile = sb("iota_tile", [P, SLOT_TILES])
        token_no = sb("token_no", [P, TILES])
        same_count = sb("same_count", [P, 1])
        same_count_u = sb("same_count_u", [P, 1], U32)
        x_hi = sb("x_hi", [P, 2, K, P], F16)
        x_lo = sb("x_lo", [P, 2, K, P], F16)

        guess = x_hi
        wh_guess = x_lo[:].rearrange("p a k n -> p (a k n)").rearrange("p (k n) -> p k n", k=K)

        at = [0]

        def carve(*shape):
            n = int(np.prod(shape))
            v = space[:, at[0]:at[0] + n]
            at[0] += n
            assert at[0] <= 2 * K * NTOK
            if len(shape) == 1:
                return v
            if len(shape) == 2:
                return v.rearrange("p (a b) -> p a b", a=shape[0])
            return v.rearrange("p (a b c) -> p a b c", a=shape[0], b=shape[1])

        hr = carve(RING, TOP, ROW)
        hidden = carve(HID)
        hiddenT = carve(Q * P).bitcast(F16).rearrange("p (s q n) -> p s q n", s=2, q=Q)
        hT_hi, hT_lo = hiddenT[:, 0], hiddenT[:, 1]
        ys = carve(RING, D)
        x_res = carve(2, D)
        slots_u = carve(TILES, TOP).bitcast(U32)
        meta = carve(TILES, TOP, 2)
        expert_u = carve(SLOT_TILES).bitcast(U32)
        slot_idx = carve(RING, TOP).bitcast(U32)
        token_idx = carve(RING).bitcast(U32)
        used_u = carve(1).bitcast(U32)
        y_scale = carve(RING)
        n_drift = K * (COLS - B)
        drift = hidden[:, 0:n_drift].rearrange("p (k n) -> p k n", k=K)
        drift_ok = hidden[:, n_drift:2 * n_drift].rearrange("p (k n) -> p k n", k=K)
        routing_at = at[0]
        xs = carve(RING, ROW)
        at[0] = routing_at
        logits = carve(TILES, E)
        best = carve(TILES, E)
        best_at = carve(TILES, E).bitcast(U32)
        chosen = carve(TOP, TILES)
        gap = carve(TILES)
        exp_gap = carve(TILES)
        denom = carve(TILES)
        onehot = carve(TOP, TILES, E)
        picked = carve(TILES, E)
        earlier = carve(E, TILES)
        per_tile = carve(E, TILES)
        running = carve(E, TILES)
        restart = carve(E, TILES)
        slot_of = carve(E, TILES)
        masked = carve(TOP * TILES, E)
        filled = carve(E, TILES)
        tiles_of = carve(E)
        tiles_upto = carve(E)
        base = carve(E)
        slots = carve(TOP, TILES)
        ended = carve(SLOT_TILES, E)
        expert_of = carve(SLOT_TILES)
        is_expert = ended
        scale_parts = space[:, routing_at:routing_at + SLOT_TILES * E].rearrange("p (t e) -> p t e", e=E)

        Z = [[ctx.enter_context(nc.psum_tensor(f"z{p}{m}", [P, BANK], F32)) for m in range(K)] for p in range(2)]
        TR = [ctx.enter_context(nc.psum_tensor(f"tr{h}", [P, BANK], F32)) for h in range(HALVES)]
        PY = ctx.enter_context(nc.psum_tensor("py", [P, BANK], F32))
        PX = ctx.enter_context(nc.psum_tensor("px", [P, BANK], F32))

        wx_in, wh_in, x_in = sem("wx_in"), sem("wh_in"), [sem(f"x_in{n}") for n in range(NTOK // BANK)]
        bias_in, h0_in, gate_in = sem("bias_in"), sem("h0_in"), sem("gate_in")
        w_in = [sem(f"w_in{f}") for f in range(FFNS)]
        bound_ok, found = sem("bound_ok"), sem("found")
        bound_all_ok, split_ok = sem("bound_all_ok"), sem("split_ok")
        x_res_in = [sem(f"x_res_in{u}") for u in range(2)]
        xs_in = [sem(f"xs_in{u}") for u in range(RING)]
        consts = sem("consts")
        identity_ok, pad_ok = sem("identity_ok"), sem("pad_ok")
        xproj_mm, xproj_ok = sem("xproj_mm"), sem("xproj_ok")
        start_ok = sem("start_ok")
        z_mm = [sem(f"z_mm{m}") for m in range(K)]
        h_ok = [sem(f"h_ok{k}") for k in range(K)]
        start_ok_general = sem("start_ok_general")
        z_mm_general = [sem(f"z_mm_general{m}") for m in range(K)]
        h_ok_general = [sem(f"h_ok_general{k}") for k in range(K)]
        drift_counted, drift_summed, drift_known = sem("drift_counted"), sem("drift_summed"), sem("drift_known")
        guess_ok = sem("guess_ok")
        x_hi_general, x_lo_general, up_mm_general = (sem(n) for n in "x_hi_general x_lo_general up_mm_general".split())
        tiles_ok = sem("tiles_ok")
        logits_mm, gap_ok, exp_ok, picked_ok, prefix_mm, prefix_read, routed = (
            sem(n) for n in "logits_mm gap_ok exp_ok picked_ok prefix_mm prefix_read routed".split())
        chain = sem("chain")
        x_hi_ok, x_lo_ok, up_mm, hidden_ok, tr_mm, h_hi_ok, h_lo_ok, down_mm, y_ok = (
            sem(n) for n in "x_hi_ok x_lo_ok up_mm hidden_ok tr_mm h_hi_ok h_lo_ok down_mm y_ok".split())
        row_mm, row_ok, row_copied = sem("row_mm"), sem("row_ok"), sem("row_copied")
        sorted_ok = [sem(f"sorted_ok{u}") for u in range(RING)]
        xs_mm, idx_ok = sem("xs_mm"), sem("idx_ok")
        summed, stored = sem("summed"), [sem(f"stored{u}") for u in range(RING)]
        added = sem("added")
        padded, padded_out = sem("padded"), sem("padded_out")
        pool_waited, sp_waited, act_waited = sem("pool_waited"), sem("sp_waited"), sem("act_waited")
        block = ctx.enter_context(nc.Block())

        GENERAL_ROUNDS = C - EXACT_ROUNDS

        def column(k, j):
            return states[:, k, bass.ds(j, 1), :].rearrange("p a n -> p (a n)")

        def weight(f, at, n, part):
            c, start = divmod(at, CHUNK)
            return w_split[:, bass.ds(f * (2 * WCOLS) + (2 * c + part) * CHUNK + start, n)]

        @block.sync
        def _(sp):
            sp.dma_start(wx_sb, wx).then_inc(wx_in, 16)
            for n in range(NTOK // BANK):
                sp.dma_start(xT[:, :, n * BANK:(n + 1) * BANK], x_cols[n]).then_inc(x_in[n], 16)
                if n == 0:
                    sp.dma_start(bias_sb[:], bias).then_inc(bias_in, 16)
            sp.dma_start(wh_sb, wh).then_inc(wh_in, 16)
            sp.dma_start(states[:, :, 0, 0:B], h0_cols).then_inc(h0_in, 16)
            sp.dma_start(gate_sb[:], gate_cols).then_inc(gate_in, 16)
            for f in range(FFNS):
                sp.dma_start(w_slots[:, f * CHUNKS + 1:(f + 1) * CHUNKS + 1].rearrange("p s c -> p (s c)"),
                             weights[f]).then_inc(w_in[f], 16)
            sp.wait_ge(pad_ok, 3)
            sp.dma_start(sorted_rows.rearrange("(t p) r -> p t r", p=P),
                         pad_row[:].unsqueeze(1).broadcast_to([P, SLOT_TILES, ROW])).then_inc(padded, 16)
            sp.dma_start(out[NTOK:NTOK + P, :], pad_row[:, 0:D]).then_inc(padded_out, 16)
            sp.wait_ge(logits_mm, 1)
            x_tiles = x_rows.rearrange("(t p) d -> t p d", p=P)
            out_tiles = out.rearrange("(t p) d -> t p d", p=P)

            def tile_of(dram, t):
                return dram[bass.ds(t, 1), :, :].rearrange("a p d -> (a p) d")

            for g in range(2):
                sp.dma_start(x_res[:, g], x_tiles[g]).then_inc(x_res_in[g], 16)

            def store(g, u, more):
                sp.wait_ge(summed, g + 1)
                sp.dma_start(tile_of(out_tiles, g), ys[:, u]).then_inc(stored[u], 16)
                if more:
                    sp.dma_start(x_res[:, u % 2], tile_of(x_tiles, g + 2)).then_inc(x_res_in[u % 2], 16)

            with sp.Fori(0, TILES // RING - 1) as i:
                for u in range(RING):
                    store(i * RING + u, u, True)
            sorted_tiles = sorted_rows.rearrange("(t p) r -> t p r", p=P)

            def load(t, u, refill):
                if refill:
                    sp.wait_ge(xs_mm, t - RING + 1)
                    sp.sem_inc(sp_waited, 1)
                    sp.wait_ge(idx_ok, t - RING + 1)
                sp.dma_start(xs[:, u], tile_of(sorted_tiles, t)).then_inc(xs_in[u], 16)

            sp.wait_ge(tiles_ok, 1)
            for u in range(RING):
                sp.wait_ge(sorted_ok[u], 16 * TOP * TILES // RING)
            for t in range(RING):
                load(t, t, False)
            for u in range(RING):
                store(TILES - RING + u, u, u < RING - 2)
            with sp.Fori(1, SLOT_TILES // RING) as i:
                for u in range(RING):
                    load(i * RING + u, u, True)
            for t in range(SLOT_TILES // RING * RING, SLOT_TILES):
                load(t, t % RING, True)
            for t in range(COMMON_TILES, SLOT_TILES):
                sp.wait_ge(xs_in[t % RING], 16 * (t // RING + 1))

        @block.gpsimd
        def _(pool):
            nc.gpsimd.memset(identity[:], 0.0).then_inc(identity_ok, 1)
            nc.gpsimd.memset(before[:], 1.0).then_inc(identity_ok, 1)
            nc.gpsimd.memset(pad_row[:], 0.0).then_inc(pad_ok, 1)
            nc.gpsimd.memset(ones[:], 1.0).then_inc(consts, 1)
            pool.wait_ge(identity_ok, 2)
            nc.gpsimd.affine_select(out=identity[:], in_=identity[:], compare_op=ALU.not_equal, fill=1.0,
                                    base=0, pattern=[[-1, P]], channel_multiplier=1).then_inc(identity_ok, 1)
            nc.gpsimd.affine_select(out=before[:], in_=before[:], compare_op=ALU.is_gt, fill=0.0,
                                    base=0, pattern=[[1, P]], channel_multiplier=-1).then_inc(consts, 1)
            for to, pattern, start, per_partition in (
                    (iota_e[:], [[1, E]], 0, 0), (iota_full[:], [[P, TILES]], 0, 0),
                    (iota_tile[:], [[1, SLOT_TILES]], 0, 0), (token_no[:], [[P, TILES]], 0, 1)):
                nc.gpsimd.iota(to, pattern=pattern, base=start, channel_multiplier=per_partition,
                               allow_small_or_imprecise_dtypes=True).then_inc(consts, 1)
            pool.wait_ge(pad_ok, 1)
            nc.gpsimd.iota(pad_row[:, D:D + 1], pattern=[[1, 1]], base=NTOK, channel_multiplier=1,
                           allow_small_or_imprecise_dtypes=True).then_inc(pad_ok, 2)

            def waited(semaphore, value):
                pool.wait_ge(semaphore, value)
                pool.sem_inc(pool_waited, 1)

            def reduce_bounds(n):
                start, end = BOUND_BATCHES[n]
                if n == 0:
                    pool.wait_ge(bound_ok, 1)
                else:
                    pool.wait_ge(found, (end - FOUND_BY_DVE) * CHUNKS)
                nc.gpsimd.partition_all_reduce(chunk_bound_all[:, start:end].rearrange("p f c -> p (f c)"),
                                               chunk_bound[:, start:end].rearrange("p f c -> p (f c)"),
                                               P, bass.bass_isa.ReduceOp.max).then_inc(bound_all_ok, 1)

            for n in range(len(BOUND_BATCHES) - 1):
                reduce_bounds(n)
            pool.wait_ge(routed, 1)

            def sort(t, u):
                waited(row_ok, t + 1)
                nc.gpsimd.tensor_copy(hr[:, u, :, D:ROW], meta[:, bass.ds(t, 1)].rearrange("p a k c -> p (a k) c")).then_inc(row_copied, 1)
                nc.gpsimd.tensor_copy(slot_idx[:, u], slots_u[:, bass.ds(t, 1)].rearrange("p a k -> p (a k)")).then_inc(row_copied, 1)
                waited(row_copied, t * 2 + 2)
                for k in range(TOP):
                    nc.gpsimd.indirect_dma_start(
                        out=sorted_rows, out_offset=bass.IndirectOffsetOnAxis(slot_idx[:, u, k:k + 1], 0),
                        in_=hr[:, u, k], in_offset=None).then_inc(sorted_ok[u], 16)

            pool.wait_ge(padded, 16)
            for t in range(RING):
                sort(t, t)
            reduce_bounds(len(BOUND_BATCHES) - 1)
            with pool.Fori(1, TILES // RING) as i:
                for u in range(RING):
                    waited(sorted_ok[u], i * (16 * TOP))
                    sort(i * RING + u, u)

            pool.wait_ge(tiles_ok, 1)
            used = pool.value_load(used_u[0:1, 0:1], min_val=1, max_val=SLOT_TILES)

            def add(t, u):
                waited(idx_ok, t + 1)
                waited(y_ok, t + (TILES + 1))
                nc.gpsimd.indirect_dma_start(
                    out=out, out_offset=bass.IndirectOffsetOnAxis(token_idx[:, u:u + 1], 0),
                    in_=ys[:, u], in_offset=None, compute_op=ALU.add).then_inc(added, 16)
                waited(added, t * 16 + 16)

            pool.wait_ge(padded_out, 16)
            for u in range(RING):
                pool.wait_ge(stored[u], 16 * TILES // RING)
            with pool.Fori(0, SLOT_TILES // RING) as i:
                for u in range(RING):
                    add(i * RING + u, u)
            for t in range(SLOT_TILES // RING * RING, COMMON_TILES):
                add(t, t % RING)
            with pool.If(used > COMMON_TILES):
                for t in range(COMMON_TILES, SLOT_TILES):
                    add(t, t % RING)

        @block.vector
        def _(dve):
            links = [0]

            def link(instruction):
                links[0] += 1
                instruction.then_inc(chain, 1)
                dve.wait_ge(chain, links[0])

            nc.vector.memset(guess[:, 0, :, B:COLS], 0.0).then_inc(guess_ok, 1)
            dve.wait_ge(wh_in, 16)
            nc.vector.tensor_scalar(wh_guess, wh_sb, MAX_F16, -MAX_F16, ALU.min, ALU.max).then_inc(guess_ok, 1)
            dve.wait_ge(h0_in, 16)
            nc.vector.tensor_scalar(guess[:, 0, :, 0:B], states[:, :, 0, 0:B], MAX_F16, -MAX_F16,
                                    ALU.min, ALU.max).then_inc(guess_ok, 1)

            def next_start(h, count, started, ends=states[:, :, L]):
                for k in range(K):
                    dve.wait_ge(h[k], count)
                nc.vector.tensor_copy(states[:, :, 0, B:COLS], ends[:, :, 0:COLS - B]).then_inc(started, 1)

            def find_largest(f):
                dve.wait_ge(w_in[f], 16)
                return nc.vector.tensor_reduce(chunk_bound[:, f], w_slots[:, f * CHUNKS + 1:(f + 1) * CHUNKS + 1],
                                               AX.X, ALU.max, apply_absolute_value=True)

            def find_scales(n):
                start, end = BOUND_BATCHES[n]
                dve.wait_ge(bound_all_ok, n + 1)
                flat = lambda v: v[:, start:end].rearrange("p f m -> p (f m)")
                link(nc.vector.tensor_reduce(flat(bound), chunk_bound_all[:, start:end].rearrange(
                    "p f (m s) -> p (f m) s", m=2), AX.X, ALU.max))
                link(nc.vector.tensor_scalar_max(flat(bound), flat(bound), LEAST_MAX))
                link(nc.vector.tensor_scalar(flat(w_pow).bitcast(U32), flat(bound).bitcast(U32),
                                             EXPONENT_MASK, None, ALU.bitwise_and))
                link(nc.vector.tensor_scalar(flat(w_scale).bitcast(U32), flat(w_pow).bitcast(U32),
                                             -1.0, SCALE_BITS, ALU.mult, ALU.add))
                nc.vector.tensor_scalar_mul(ffn_scales[:, 0, start:end], w_pow[:, start:end, 0], UP_UNSCALE)
                nc.vector.tensor_scalar_mul(ffn_scales[:, 1, start:end], w_scale[:, start:end, 0], HIDDEN_SCALE)
                link(nc.vector.scalar_tensor_tensor(ffn_scales[:, 2, start:end], w_pow[:, start:end, 0],
                                                    DOWN_UNSCALE, w_pow[:, start:end, 1], ALU.mult, ALU.mult))

            def split(c):
                f, m = c // CHUNKS, c % CHUNKS // (CHUNKS // 2)
                high, low = (w_split[:, (2 * c + part) * CHUNK:(2 * c + part + 1) * CHUNK] for part in range(2))
                scale = w_scale[:, f, m:m + 1]
                if c:
                    dve.wait_ge(split_ok, c)
                link(nc.vector.tensor_scalar(high, w_slots[:, c + 1], scale, None, ALU.mult))
                nc.vector.scalar_tensor_tensor(low, w_slots[:, c + 1], scale, high, ALU.mult, ALU.subtract).then_inc(split_ok, 1)

            def split_upto(end):
                for c in range(split_done[0], end):
                    split(c)
                split_done[0] = end

            split_done = [0]
            for f in range(FOUND_BY_DVE):
                last = find_largest(f)
            last.then_inc(bound_ok, 1)
            find_scales(0)
            link(nc.vector.tensor_copy(tile_scales[:, 0:TILES].rearrange("p t s -> p s t"),
                                       ffn_scales[:, :, 0:1].broadcast_to([P, 3, TILES])))
            split_upto(CHUNKS // 2 + 1)
            next_start(h_ok, L, start_ok, ends=guess[:, L % 2])
            split_upto(2 * CHUNKS)
            find_scales(1)
            split_upto(2 * CHUNKS + 6)
            next_start(h_ok, 2 * L, start_ok)
            find_scales(2)
            split_upto(4 * CHUNKS)
            find_scales(3)
            split_upto(EARLY_CHUNKS)

            def states_low(g, source, p, ready=x_hi_ok, done=x_lo_ok):
                dve.wait_ge(ready, g + 1)
                nc.vector.scalar_tensor_tensor(x_lo[:, p], source, STATE_SCALE, x_hi[:, p],
                                               ALU.mult, ALU.subtract).then_inc(done, 1)

            def shared_states(g):
                return states[:, :, bass.ds(g + 1, 1), :].rearrange("p k a n -> p k (a n)")

            for g in range(2):
                states_low(g, shared_states(g), g)

            for k in range(K):
                dve.wait_ge(h_ok[k], SPECULATIVE_ROUNDS * L)
            link(nc.vector.tensor_sub(drift, states[:, :, L, 0:COLS - B], states[:, :, 0, B:COLS]))
            link(nc.vector.tensor_mul(drift_ok, drift, drift))
            link(nc.vector.tensor_scalar(drift, drift_ok, TOLERANCE ** 2, None, ALU.is_le))
            nc.vector.tensor_reduce(same_count[:], drift, AX.XY, ALU.add).then_inc(drift_counted, 1)
            dve.wait_ge(drift_summed, 1)
            nc.vector.tensor_copy(same_count_u[:], PY[:, 0:1]).then_inc(drift_known, 1)
            dve.wait_ge(drift_known, 1)
            same = dve.value_load(same_count_u[0:1, 0:1], min_val=0, max_val=EXPECTED_SAME)
            with dve.If(same != EXPECTED_SAME):
                next_start(h_ok, SPECULATIVE_ROUNDS * L, start_ok_general)
                with dve.Fori(1, GENERAL_ROUNDS) as r:
                    next_start(h_ok_general, r * L, start_ok_general)
                for g in range(2):
                    states_low(g, shared_states(g), g, x_hi_general, x_lo_general)
            dve.engine_nop()

            def hidden_low(g):
                for h in range(HALVES):
                    dve.wait_ge(h_hi_ok, g * HALVES + (h + 1))
                    part = slice(h * TPB, (h + 1) * TPB)
                    nc.vector.scalar_tensor_tensor(
                        hT_lo[:, part].rearrange("p q n -> p (q n)"), TR[h][:],
                        tile_scales[:, bass.ds(g, 1), 1:2].rearrange("p a n -> p (a n)"),
                        hT_hi[:, part].rearrange("p q n -> p (q n)"), ALU.mult, ALU.subtract).then_inc(h_lo_ok, 1)

            def residual(g):
                u = g % RING
                dve.wait_ge(x_res_in[u % 2], 16 * (g // 2 + 1))
                dve.wait_ge(y_ok, g + 1)
                nc.vector.tensor_add(ys[:, u], ys[:, u], x_res[:, u % 2]).then_inc(summed, 1)

            def index(t, u, n, again):
                dve.wait_ge(xs_in[u], n)
                if again:
                    dve.wait_ge(added, (t - RING + 1) * 16)
                nc.vector.tensor_copy(token_idx[:, u:u + 1], xs[:, u, D:D + 1])
                nc.vector.tensor_mul(y_scale[:, u:u + 1], xs[:, u, D + 1:D + 2],
                                     tile_scales[:, bass.ds(t + TILES, 1), 2:3].rearrange("p a n -> p (a n)")).then_inc(idx_ok, 1)

            def route_gap():
                dve.wait_ge(logits_mm, 1)
                link(nc.vector.tensor_copy(logits, PX[:, 0:TILES * E].rearrange("p (t e) -> p t e", e=E)))
                for t in range(TILES):
                    last = nc.vector.max(best[:, t], logits[:, t])
                link(last)
                nc.vector.tensor_sub(gap, best[:, :, 1], best[:, :, 0]).then_inc(gap_ok, 1)

            def route_choice():
                for t in range(TILES):
                    last = nc.vector.max_index(best_at[:, t], best[:, t], logits[:, t])
                link(last)
                for k in range(TOP):
                    last = nc.vector.tensor_copy(chosen[:, k], best_at[:, :, k])
                link(last)
                dve.wait_ge(consts, 6)
                for k in range(TOP):
                    last = nc.vector.tensor_tensor(
                        onehot[:, k], chosen[:, k].unsqueeze(2).broadcast_to([P, TILES, E]),
                        iota_e[:].unsqueeze(1).broadcast_to([P, TILES, E]), ALU.is_equal)
                link(last)
                nc.vector.tensor_add(picked, onehot[:, 0], onehot[:, 1]).then_inc(picked_ok, 1)
                link(nc.vector.memset(restart, 1.0))
                link(nc.vector.memset(restart[:, :, 0:1], 0.0))

            def route_gates():
                dve.wait_ge(exp_ok, 1)
                link(nc.vector.tensor_scalar_add(denom, exp_gap, 1.0))
                link(nc.vector.reciprocal(meta[:, :, 0, 1], denom))
                nc.vector.tensor_mul(meta[:, :, 1, 1], exp_gap, meta[:, :, 0, 1])
                for k in range(TOP):
                    nc.vector.tensor_copy(meta[:, :, k, 0], token_no[:])

            def route_slots():
                dve.wait_ge(prefix_mm, 1)
                nc.vector.tensor_copy(earlier, PX[:, P:2 * P].rearrange("p (t e) -> p e t", e=E))
                prefix = nc.vector.tensor_copy(per_tile, PX[:, 2 * P:3 * P].rearrange("p (t e) -> p e t", e=E))
                prefix.then_inc(prefix_read, 1)
                dve.wait_ge(prefix_read, 1)
                flat = lambda v: v.rearrange("p e t -> p (e t)")
                link(nc.vector.tensor_tensor_scan(flat(running), flat(restart), flat(per_tile), 0.0, ALU.mult, ALU.add))
                link(nc.vector.tensor_tensor(filled, running[:, :, TILES - 1:TILES].broadcast_to([P, E, TILES]),
                                             iota_full[:].unsqueeze(1).broadcast_to([P, E, TILES]), ALU.is_gt))
                link(nc.vector.tensor_reduce(tiles_of, filled, AX.X, ALU.add))
                link(nc.vector.tensor_tensor_scan(tiles_upto, ones[:, 0:E], tiles_of, 0.0, ALU.mult, ALU.add))
                nc.vector.tensor_copy(used_u, tiles_upto[:, E - 1:E])
                nc.vector.tensor_tensor(ended, tiles_upto.unsqueeze(1).broadcast_to([P, SLOT_TILES, E]),
                                        iota_tile[:].unsqueeze(2).broadcast_to([P, SLOT_TILES, E]), ALU.is_le)
                link(nc.vector.tensor_sub(base, tiles_upto, tiles_of))
                link(nc.vector.tensor_scalar_mul(tiles_upto, base, float(P)))
                link(nc.vector.tensor_sub(slot_of, running, per_tile))
                link(nc.vector.tensor_add(slot_of, slot_of, earlier))
                link(nc.vector.tensor_add(slot_of, slot_of, tiles_upto.unsqueeze(2).broadcast_to([P, E, TILES])))
                for k in range(TOP):
                    last = nc.vector.tensor_mul(masked[:, k * TILES:(k + 1) * TILES], onehot[:, k], slot_of.rearrange("p e t -> p t e"))
                link(last)
                link(nc.vector.tensor_reduce(slots.rearrange("p k t -> p (k t)"), masked, AX.X, ALU.add))
                for k in range(TOP):
                    last = nc.vector.tensor_copy(slots_u[:, :, k], slots[:, k])
                last.then_inc(routed, 1)

            def route_tiles():
                link(nc.vector.tensor_reduce(expert_of, ended, AX.X, ALU.add))
                link(nc.vector.tensor_scalar_min(expert_of, expert_of, float(E - 1)))
                nc.vector.tensor_scalar_add(expert_u, expert_of, 1.0)
                link(nc.vector.tensor_tensor(is_expert, expert_of.unsqueeze(2).broadcast_to([P, SLOT_TILES, E]),
                                             iota_e[:].unsqueeze(1).broadcast_to([P, SLOT_TILES, E]), ALU.is_equal))
                for n in range(3):
                    link(nc.vector.tensor_mul(scale_parts, is_expert,
                                              ffn_scales[:, n, 1:FFNS].unsqueeze(1).broadcast_to([P, SLOT_TILES, E])))
                    last = nc.vector.tensor_reduce(tile_scales[:, TILES:ALL_TILES, n], scale_parts, AX.X, ALU.add)
                    if n < 2:
                        link(last)
                last.then_inc(tiles_ok, 1)

            route_gap()
            route_choice()
            for g in range(TILES):
                hidden_low(g)
                if g + 2 < TILES:
                    states_low(g + 2, shared_states(g + 2), g % 2)
                else:
                    states_low(g + 2, PX[:, 0:D].rearrange("p (k n) -> p k n", k=K), g % 2)
                if g >= 1:
                    residual(g - 1)
                if g == 0:
                    route_gates()
                elif g == 1:
                    route_slots()
                elif g == FIND_TILES:
                    find_scales(5)
                    route_tiles()
                elif g < TILES - 1:
                    if g == 3:
                        find_scales(4)
                    scaled = BOUND_BATCHES[4][0] * CHUNKS
                    rounds = g - 2 if g < FIND_TILES else g - 3
                    split_upto(scaled if g == 2 else
                               scaled + -(-(FFNS * CHUNKS - scaled) * rounds // (TILES - 5)))
            residual(TILES - 1)
            index(0, 0, 16, False)

            def expert(t, u, n, again, fetch=True, index_next=True):
                hidden_low(t + TILES)
                if fetch:
                    states_low(t + (TILES + 2), PX[:, 0:D].rearrange("p (k n) -> p k n", k=K), u % 2)
                if index_next:
                    index(t + 1, (u + 1) % RING, n, again)

            for t in range(RING):
                expert(t, t, 16 * ((t + 1) // RING + 1), t + 1 >= RING)
            with dve.Fori(1, SLOT_TILES // RING) as i:
                for u in range(RING):
                    expert(i * RING + u, u, i * 16 + 16 * ((u + 1) // RING + 1), True)
            for t in range(SLOT_TILES // RING * RING, COMMON_TILES):
                expert(t, t % RING, 16 * ((t + 1) // RING + 1), True, fetch=False, index_next=t + 1 < COMMON_TILES)
            used = dve.value_load(used_u[0:1, 0:1], min_val=1, max_val=SLOT_TILES)
            with dve.If(used > COMMON_TILES):
                t = COMMON_TILES
                index(t, t % RING, 16 * (t // RING + 1), True)
                states_low(t + 1 + TILES, PX[:, 0:D].rearrange("p (k n) -> p k n", k=K), (t + 1) % 2)
                for t in range(COMMON_TILES, SLOT_TILES):
                    expert(t, t % RING, 16 * ((t + 1) // RING + 1), True, fetch=False, index_next=t + 1 < SLOT_TILES)

        @block.scalar
        def _(act):
            act.wait_ge(bias_in, 16)
            for n in range(NTOK // BANK):
                for m in range(K):
                    act.wait_ge(xproj_mm, n * K + m + 1)
                    nc.scalar.activation(xproj[:, m, n * BANK:(n + 1) * BANK], Z[n % 2][m][:], ACT.Identity,
                                         bias=bias_sb[:, m:m + 1]).then_inc(xproj_ok, 1)

            def find_bound(c):
                nc.scalar.activation(magnitudes[:], w_slots[:, bass.ds(c + 1, 1), :].rearrange("p a c -> p (a c)"), ACT.Abs,
                                     accum_out=chunk_bound[:].rearrange("p f c -> p (f c)")[:, bass.ds(c, 1)]).then_inc(found, 1)

            def step_pair(z, h, r, i, find_at=None):
                for u in range(2):
                    for m in range(K):
                        act.wait_ge(z[m], i * 2 + (r * L + u + 1))
                        nc.scalar.activation(column(m, i * 2 + u + 1), Z[u][m][:, 0:COLS], ACT.Tanh).then_inc(h[m], 1)
                    if find_at is not None:
                        act.wait_ge(h[0], i * 2 + (r * L + u + 1))
                        find_bound(i * 2 + (find_at + u))

            def shared_rows(g, u, done):
                nc.scalar.mul(x_hi[:, u % 2], states[:, :, bass.ds(g + 1, 1), :].rearrange("p k a n -> p k (a n)"),
                              STATE_SCALE).then_inc(done, 1)

            with act.Fori(0, L // 2) as i:
                for u in range(2):
                    for m in range(K):
                        act.wait_ge(z_mm[m], i * 2 + (u + 1))
                        nc.scalar.activation(guess[:, 1 - u, m], Z[u][m][:, 0:COLS], ACT.Tanh).then_inc(h_ok[m], 1)
            for r in range(1, SPECULATIVE_ROUNDS):
                find_at = (FOUND_BY_DVE - 2) * CHUNKS + r * L
                for half in range(2):
                    act.wait_ge(w_in[find_at // CHUNKS + half], 16)
                    final = r == SPECULATIVE_ROUNDS - 1 and half == 1
                    with act.Fori(half * L // 4, (half + 1) * L // 4 - final) as i:
                        step_pair(z_mm, h_ok, r, i, find_at)
            for k in range(K):
                act.wait_ge(h_ok[k], r * L + 2)
            for g in range(2):
                shared_rows(g, g, x_hi_ok)
            step_pair(z_mm, h_ok, r, L // 2 - 1, find_at)
            act.wait_ge(drift_known, 1)
            same = act.value_load(same_count_u[0:1, 0:1], min_val=0, max_val=EXPECTED_SAME)
            with act.If(same != EXPECTED_SAME):
                with act.Fori(0, GENERAL_ROUNDS) as r:
                    with act.Fori(0, L // 2) as i:
                        step_pair(z_mm_general, h_ok_general, r, i)
                for k in range(K):
                    act.wait_ge(h_ok_general[k], GENERAL_ROUNDS * L)
                for g in range(2):
                    shared_rows(g, g, x_hi_general)
                act.wait_ge(up_mm_general, HALVES)

            act.wait_ge(gap_ok, 1)
            nc.scalar.activation(exp_gap, gap, ACT.Exp).then_inc(exp_ok, 1)

            def tile_scale(g, n):
                return tile_scales[:, bass.ds(g, 1), n:n + 1].rearrange("p a n -> p (a n)")

            def silu(g, p):
                for h in range(HALVES):
                    act.wait_ge(up_mm, g * HALVES + (h + 1))
                    if h == 0 and not (isinstance(g, int) and g == 0):
                        act.wait_ge(tr_mm, g * HALVES)
                    act.sem_inc(act_waited, 1)
                    nc.scalar.activation(hidden[:, h * BANK:(h + 1) * BANK], Z[p][h][:], ACT.Silu,
                                         scale=tile_scale(g, 0)).then_inc(hidden_ok, 1)

            def transposed(g):
                for h in range(HALVES):
                    act.wait_ge(tr_mm, g * HALVES + (h + 1))
                    if h == 0 and not (isinstance(g, int) and g == 0):
                        act.wait_ge(down_mm, g)
                    act.sem_inc(act_waited, 1)
                    nc.scalar.mul(hT_hi[:, h * TPB:(h + 1) * TPB].rearrange("p q n -> p (q n)"), TR[h][:],
                                  tile_scale(g, 1)).then_inc(h_hi_ok, 1)

            def sorted_in(t, p):
                act.wait_ge(xs_mm, t + 1)
                nc.scalar.mul(x_hi[:, p].rearrange("p k n -> p (k n)"), PX[:, 0:D], STATE_SCALE).then_inc(x_hi_ok, 1)

            def free_ys(g, u, stores, adds):
                if stores is not None:
                    act.wait_ge(stored[u], stores)
                if adds is not None:
                    act.wait_ge(added, adds)

            def iteration(g, u, phase, silu_next=True, sort=None, fetch="shared", stores=None, adds=None, find=False):
                def sort_row(v):
                    t, s, again = sort
                    act.wait_ge(row_mm, t + (v + 1))
                    if again is not None:
                        act.wait_ge(sorted_ok[s + v], again)
                    nc.scalar.copy(hr[:, s + v, :, 0:D],
                                   PX[:, 0:D].unsqueeze(1).broadcast_to([P, TOP, D])).then_inc(row_ok, 1)

                if sort is not None:
                    sort_row(0)
                transposed(g)
                if silu_next:
                    silu(g + 1, (u + 1) % 2)
                if fetch == "shared":
                    act.wait_ge(up_mm, (g + 1) * HALVES)
                    shared_rows(g + 2, u, x_hi_ok)
                elif fetch == "sorted":
                    act.wait_ge(up_mm, (g + 1) * HALVES)
                    sorted_in(g + (2 - TILES), u % 2)
                if sort is not None:
                    sort_row(1)
                if find:
                    for c in range(FOUND_LATE * CHUNKS + g * FINDS, FOUND_LATE * CHUNKS + (g + 1) * FINDS):
                        act.wait_ge(w_in[c // CHUNKS], 16)
                        act.wait_ge(found, c - FOUND_BY_DVE * CHUNKS)
                        find_bound(c)
                act.wait_ge(down_mm, g + 1)
                free_ys(g, u, stores, adds)
                if phase == "shared":
                    nc.scalar.mul(ys[:, u], PY[:, 0:D], tile_scale(g, 2)).then_inc(y_ok, 1)
                else:
                    act.wait_ge(idx_ok, g - (TILES - 1))
                    nc.scalar.mul(ys[:, u], PY[:, 0:D], y_scale[:, u:u + 1]).then_inc(y_ok, 1)

            act.wait_ge(split_ok, 1)
            silu(0, 0)
            for g in range(RING):
                iteration(g, g, "shared", find=True)
            for g in range(SORT_FROM, SORT_FROM + SORT_TILES):
                t = 2 * (g - SORT_FROM)
                u = g % RING
                iteration(g, u, "shared", sort=(t, t % RING, None if t < RING else 16 * TOP * (t // RING)),
                          stores=16 * (g // RING), find=g < FIND_TILES)
            act.wait_ge(tiles_ok, 1)
            for g in range(SORT_FROM + SORT_TILES, TILES):
                u = g % RING
                iteration(g, u, "shared", fetch="shared" if g + 2 < TILES else "sorted", stores=16 * (g // RING))
            for u in range(RING):
                iteration(TILES + u, u, "sorted", fetch="sorted", stores=16 * (TILES // RING))
            with act.Fori(1, SLOT_TILES // RING) as i:
                for u in range(RING):
                    iteration(i * RING + (TILES + u), u, "sorted", fetch="sorted", adds=i * (16 * RING) + 16 * (u + 1 - RING))
            def last_iteration(t, end):
                iteration(TILES + t, t % RING, "sorted", silu_next=t + 1 < end, fetch=None, adds=16 * (t - RING + 1))

            for t in range(SLOT_TILES // RING * RING, COMMON_TILES):
                last_iteration(t, COMMON_TILES)
            used = act.value_load(used_u[0:1, 0:1], min_val=1, max_val=SLOT_TILES)
            with act.If(used > COMMON_TILES):
                sorted_in(COMMON_TILES + 1, (COMMON_TILES + 1) % 2)
                silu(TILES + COMMON_TILES, COMMON_TILES % 2)
                for t in range(COMMON_TILES, SLOT_TILES):
                    last_iteration(t, SLOT_TILES)

        @block.tensor
        def _(pe):
            pe.wait_ge(wx_in, 16)
            for n in range(NTOK // BANK):
                pe.wait_ge(x_in[n], 16)
                for m in range(K):
                    if n >= 2:
                        pe.wait_ge(xproj_ok, (n - 2) * K + m + 1)
                    for k in range(K):
                        last = nc.tensor.matmul(Z[n % 2][m][:], wx_sb[:, k, m * P:(m + 1) * P],
                                                xT[:, k, n * BANK:(n + 1) * BANK], start=k == 0, stop=k == K - 1)
                    last.then_inc(xproj_mm, 1)
            pe.wait_ge(identity_ok, 3)
            pe.wait_ge(wh_in, 16)
            pe.wait_ge(h0_in, 16)
            pe.wait_ge(xproj_ok, K * NTOK // BANK)

            def inject(p, j):
                for m in range(K):
                    nc.tensor.matmul(Z[p][m][:, 0:COLS], identity[:], xproj[:, m, bass.ds(j * COLS, COLS)],
                                     start=True, stop=False)

            def router(start, end):
                for t in range(start, end):
                    for k in range(K):
                        last = nc.tensor.matmul(PX[:, t * E:(t + 1) * E], states[:, k, t + 1], gate_sb[:, k],
                                                start=k == 0, stop=k == K - 1)
                return last

            def up_half(p, f, h, done):
                for k in range(K):
                    for x, part in ((x_hi, 0), (x_hi, 1), (x_lo, 0)):
                        last = nc.tensor.matmul(Z[p][h][:], x[:, p, k], weight(f, k * HID + h * BANK, BANK, part),
                                                start=k == 0 and x is x_hi and part == 0,
                                                stop=k == K - 1 and x is x_lo)
                last.then_inc(done, 1)

            def pair(z, h, r, i, first, final, route=False, guessing=False):
                for u in range(2):
                    for k in range(K):
                        if not (first and u == 0):
                            pe.wait_ge(h[k], i * 2 + (r * L + u))
                        for m in range(K):
                            w, state = (wh_guess, guess[:, u, k]) if guessing else (wh_sb, column(k, i * 2 + u))
                            last = nc.tensor.matmul(Z[u][m][:, 0:COLS], w[:, k, m * P:(m + 1) * P], state,
                                                    start=False, stop=k == K - 1)
                            if k == K - 1:
                                last.then_inc(z[m], 1)
                    if not (final and u == 1):
                        inject(1 - u, i * 2 + u + 1)
                    if route and i * 2 + u:
                        router(i * 2 + u - 1, i * 2 + u)

            def round_(z, h, r, guessing=False):
                pair(z, h, r, 0, True, False, guessing=guessing)
                with pe.Fori(1, L // 2 - 1) as i:
                    pair(z, h, r, i, False, False, guessing=guessing)
                pair(z, h, r, L // 2 - 1, False, True, guessing=guessing)

            inject(0, 0)
            pe.wait_ge(guess_ok, 3)
            round_(z_mm, h_ok, 0, guessing=True)
            for r in range(1, SPECULATIVE_ROUNDS - 1):
                inject(0, 0)
                pe.wait_ge(start_ok, r)
                round_(z_mm, h_ok, r)
            pe.wait_ge(gate_in, 16)
            inject(0, 0)
            pe.wait_ge(start_ok, SPECULATIVE_ROUNDS - 1)
            for i in range(L // 2):
                pair(z_mm, h_ok, SPECULATIVE_ROUNDS - 1, i, i == 0, i == L // 2 - 1, route=True)
            pe.wait_ge(split_ok, CHUNKS)
            pe.wait_ge(x_hi_ok, 1)
            pe.wait_ge(x_lo_ok, 1)
            up_half(0, SHARED, 0, up_mm)
            pe.wait_ge(drift_counted, 1)
            pe.wait_ge(consts, 6)
            nc.tensor.matmul(PY[:, 0:1], ones[:], same_count[:], start=True, stop=True).then_inc(drift_summed, 1)
            up_half(0, SHARED, 1, up_mm)
            pe.wait_ge(drift_known, 1)
            same = pe.value_load(same_count_u[0:1, 0:1], min_val=0, max_val=EXPECTED_SAME)
            with pe.If(same != EXPECTED_SAME):
                for h in range(HALVES):
                    pe.wait_ge(up_mm, h + 1)
                with pe.Fori(0, GENERAL_ROUNDS) as r:
                    inject(0, 0)
                    pe.wait_ge(start_ok_general, r + 1)
                    round_(z_mm_general, h_ok_general, r)
                for k in range(K):
                    pe.wait_ge(h_ok_general[k], GENERAL_ROUNDS * L)
                router(0, TILES - 1)
                pe.wait_ge(x_hi_general, 2)
                pe.wait_ge(x_lo_general, 2)
                for h in range(HALVES):
                    up_half(0, SHARED, h, up_mm_general)
            for k in range(K):
                pe.wait_ge(h_ok[k], SPECULATIVE_ROUNDS * L)
            router(TILES - 1, TILES).then_inc(logits_mm, 1)

            def up(g, p, f, first=False):
                pe.wait_ge(x_hi_ok, g + 1)
                pe.wait_ge(x_lo_ok, g + 1)
                if not first:
                    pe.wait_ge(hidden_ok, (g - 1) * HALVES)
                for h in range(HALVES):
                    up_half(p, f, h, up_mm)

            def turn(g, first=False):
                for h in range(HALVES):
                    pe.wait_ge(hidden_ok, g * HALVES + (h + 1))
                    if not first:
                        pe.wait_ge(h_lo_ok, (g - 1) * HALVES + (h + 1))
                    for q in range(TPB):
                        last = nc.tensor.transpose(TR[h][:, q * P:(q + 1) * P],
                                                   hidden[:, (h * TPB + q) * P:(h * TPB + q + 1) * P], identity[:])
                    last.then_inc(tr_mm, 1)

            def down(g, f, first=False):
                if not first:
                    pe.wait_ge(y_ok, g)
                for x, ready in ((hT_hi, h_hi_ok), (hT_lo, h_lo_ok)):
                    for q in range(Q):
                        if q % TPB == 0:
                            pe.wait_ge(ready, g * HALVES + (q // TPB + 1))
                        for part in range(2 if x is hT_hi else 1):
                            last = nc.tensor.matmul(PY[:, 0:D], x[:, q], weight(f, MATRIX + q * D, D, part),
                                                    start=q == 0 and x is hT_hi and part == 0,
                                                    stop=q == Q - 1 and x is hT_lo)
                last.then_inc(down_mm, 1)

            def sorted_columns(t, u, n):
                pe.wait_ge(xs_in[u], n)
                pe.wait_ge(x_lo_ok, t + TILES)
                for k in range(K):
                    last = nc.tensor.transpose(PX[:, k * P:(k + 1) * P], xs[:, u, k * P:(k + 1) * P], identity[:])
                last.then_inc(xs_mm, 1)

            def rows(t):
                if t:
                    pe.wait_ge(row_ok, t)
                for k in range(K):
                    last = nc.tensor.transpose(PX[:, k * P:(k + 1) * P], states[:, k, t + 1], identity[:])
                last.then_inc(row_mm, 1)

            up(1, 1, SHARED, first=True)
            turn(0, first=True)
            pe.wait_ge(picked_ok, 1)
            for n, m in enumerate((before, ones)):
                last = nc.tensor.matmul(PX[:, (n + 1) * P:(n + 2) * P], m[:], picked.rearrange("p t e -> p (t e)"),
                                        start=True, stop=True)
            last.then_inc(prefix_mm, 1)
            down(0, SHARED, first=True)
            for g in range(1, RING):
                turn(g)
                up(g + 1, (g + 1) % 2, SHARED)
                down(g, SHARED)
            pe.wait_ge(prefix_read, 1)
            for g in range(SORT_FROM, SORT_FROM + SORT_TILES):
                rows(2 * (g - SORT_FROM))
                turn(g)
                up(g + 1, (g + 1) % 2, SHARED)
                rows(2 * (g - SORT_FROM) + 1)
                down(g, SHARED)
            pe.wait_ge(tiles_ok, 1)
            pe.wait_ge(row_ok, TILES)

            def expert(t):
                return pe.value_load(expert_u[0:1, bass.ds(t, 1)], min_val=1, max_val=E)

            for g in range(SORT_FROM + SORT_TILES, TILES - 2):
                turn(g)
                up(g + 1, (g + 1) % 2, SHARED)
                down(g, SHARED)
            turn(TILES - 2)
            up(TILES - 1, 1, SHARED)
            sorted_columns(0, 0, 16)
            down(TILES - 2, SHARED)
            first_expert = expert(0)
            turn(TILES - 1)
            pe.wait_ge(split_ok, FFNS * CHUNKS)
            up(TILES, 0, first_expert)
            sorted_columns(1, 1, 16)
            down(TILES - 1, SHARED)

            def iteration(t, u, n_in, up_next=True, fetch=True):
                turn(TILES + t)
                if up_next:
                    up(TILES + t + 1, (u + 1) % 2, expert(t + 1))
                if fetch:
                    sorted_columns(t + 2, (u + 2) % RING, n_in)
                down(TILES + t, expert(t))

            with pe.Fori(0, SLOT_TILES // RING) as i:
                for u in range(RING):
                    iteration(i * RING + u, u, i * 16 + 16 * (1 + (u + 2) // RING))
            for t in range(SLOT_TILES // RING * RING, COMMON_TILES):
                iteration(t, t % RING, 0, up_next=t + 1 < COMMON_TILES, fetch=False)
            used = pe.value_load(used_u[0:1, 0:1], min_val=1, max_val=SLOT_TILES)
            with pe.If(used > COMMON_TILES):
                t = COMMON_TILES
                up(TILES + t, t % 2, expert(t))
                sorted_columns(t + 1, (t + 1) % RING, 16 * ((t + 1) // RING + 1))
                for t in range(COMMON_TILES, SLOT_TILES):
                    iteration(t, t % RING, 0, up_next=t + 1 < SLOT_TILES, fetch=False)


def kernel(**inputs):
    import numpy as _np
    import concourse.bacc as _bacc
    from concourse import mybir as _mybir
    from concourse.bass_utils import run_bass_kernel_spmd as _run

    a = {n: _np.asarray(v) for n, v in inputs.items()}
    x = a["x"].reshape(B, C, L, D)
    w1 = _np.concatenate([a["L0_ffn_shared_w1"][None], a["L0_ffn_experts_w1"]])
    w2 = _np.concatenate([a["L0_ffn_shared_w2"][None], a["L0_ffn_experts_w2"]])
    w1 = w1.reshape(E + 1, HID, K, P).transpose(0, 3, 2, 1).reshape(E + 1, P, K * HID)
    w2 = w2.reshape(E + 1, D, Q, P).transpose(0, 3, 2, 1).reshape(E + 1, P, Q * D)
    laid = {
        "x_cols": x.transpose(3, 2, 1, 0).reshape(K, P, NTOK // BANK, BANK).transpose(2, 1, 0, 3),
        "x_rows": x.transpose(2, 1, 0, 3).reshape(NTOK, D),
        "h0_cols": a["cond_1024"].reshape(B, K, P).transpose(2, 1, 0),
        "wx": a["L0_cond_Wx"].reshape(K, P, D).transpose(1, 0, 2),
        "wh": a["L0_cond_Wh"].reshape(K, P, D).transpose(1, 0, 2),
        "bias": a["L0_cond_b"].reshape(K, P).T,
        "weights": _np.concatenate([w1, w2], axis=2),
        "gate_cols": a["L0_ffn_gate_w"].reshape(E, K, P).transpose(2, 1, 0),
    }
    nc = _bacc.Bacc("TRN2", target_bir_lowering=False, num_devices=1)
    arrays, args = {}, []
    for name, v in laid.items():
        arrays[name] = _np.ascontiguousarray(v)
        args.append(nc.dram_tensor(name, v.shape, _mybir.dt.from_np(v.dtype), kind="ExternalInput").ap())
    rows = NTOK + P
    args.append(nc.dram_tensor("out", (rows, D), F32, kind="ExternalOutput").ap())
    build(nc, *args)
    r = _run(nc, [arrays], core_ids=[0])
    got = r.results[0]["out"][:NTOK]
    return got.reshape(L, C, B, D).transpose(2, 1, 0, 3).reshape(B, T, D)
```
